# Optimizing a Trainium2 kernel written in Bass

```python
import numpy as np
import jax
import jax.numpy as jnp

def _softmax(x, axis=-1):
    return jax.nn.softmax(x, axis=axis)

def _gelu(x):
    return jax.nn.gelu(x, approximate=True)

def _silu(x):
    return jax.nn.silu(x)

def _sigmoid(x):
    return jax.nn.sigmoid(x)

def _layernorm(x, axis=-1, eps=1e-05):
    m = jnp.mean(x, axis=axis, keepdims=True)
    v = jnp.var(x, axis=axis, keepdims=True)
    return (x - m) / jnp.sqrt(v + eps)

def _scatter_add(tgt, idx, src, axis=0):
    return tgt.at[idx].add(src)

def _segment_sum(src, seg, n):
    return jax.ops.segment_sum(src, seg, n)
kernel_name = 'mk_sandwich_d1_jaxref_r8_2f93e9'

def setup_inputs(seed: int=0):
    np.random.seed(seed)
    _w = jnp.asarray

    def _L0_attn_setup():
        import math
        import jax, jax.numpy as jnp
        import numpy as np
        N_HEAD = 16
        key = jax.random.key(seed)
        k1, k2, k3, k4 = jax.random.split(key, 4)
        B, T, C, R = (4, 256, 128, 64)
        std = 0.02
        return {'hidden_states': jax.random.normal(k1, (B, T, C), dtype=jnp.float32), 'W_basis': jax.random.normal(k2, (R, C), dtype=jnp.float32) * std, 'W_v': jax.random.normal(k3, (C, C), dtype=jnp.float32) * std, 'b_v': jnp.zeros((C,), dtype=jnp.float32), 'W_o': jax.random.normal(k4, (C, C), dtype=jnp.float32) * std, 'b_o': jnp.zeros((C,), dtype=jnp.float32)}
    _L0_attn_in = _L0_attn_setup()

    def _L0_ffn_setup():
        import jax, jax.numpy as jnp
        import numpy as np
        D_IN, D_HID = (128, 512)

        def _ternary(key, shape):
            return jax.random.randint(key, shape, -1, 2).astype(jnp.float32)

        def _tlin(x, w, s):
            return jnp.einsum('bsi,oi->bso', x, w) * s
        key = jax.random.key(seed)
        ks = jax.random.split(key, 12)
        inv = lambda fan: 1.0 / np.sqrt(fan).astype(np.float32)
        return {'x': jax.random.normal(ks[0], (4, 256, D_IN), dtype=jnp.float32), 'w1_w': _ternary(ks[1], (D_HID, D_IN)), 'w1_s': jax.random.uniform(ks[2], (D_HID,), dtype=jnp.float32) * inv(D_IN), 'w2_w': _ternary(ks[3], (D_HID, D_IN)), 'w2_s': jax.random.uniform(ks[4], (D_HID,), dtype=jnp.float32) * inv(D_IN), 'h1_w': _ternary(ks[5], (D_HID, D_HID)), 'h1_s': jax.random.uniform(ks[6], (D_HID,), dtype=jnp.float32) * inv(D_HID), 'h2_w': _ternary(ks[7], (D_HID, D_HID)), 'h2_s': jax.random.uniform(ks[8], (D_HID,), dtype=jnp.float32) * inv(D_HID), 'w3_w': _ternary(ks[9], (D_IN, D_HID)), 'w3_s': jax.random.uniform(ks[10], (D_IN,), dtype=jnp.float32) * inv(D_HID)}
    _L0_ffn_in = _L0_ffn_setup()
    _d = {'L0_attn_hidden_states': _L0_attn_in['hidden_states'], 'L0_attn_W_basis': _L0_attn_in['W_basis'], 'L0_attn_W_v': _L0_attn_in['W_v'], 'L0_attn_b_v': _L0_attn_in['b_v'], 'L0_attn_W_o': _L0_attn_in['W_o'], 'L0_attn_b_o': _L0_attn_in['b_o'], 'L0_ffn_w1_w': _L0_ffn_in['w1_w'], 'L0_ffn_w1_s': _L0_ffn_in['w1_s'], 'L0_ffn_w2_w': _L0_ffn_in['w2_w'], 'L0_ffn_w2_s': _L0_ffn_in['w2_s'], 'L0_ffn_h1_w': _L0_ffn_in['h1_w'], 'L0_ffn_h1_s': _L0_ffn_in['h1_s'], 'L0_ffn_h2_w': _L0_ffn_in['h2_w'], 'L0_ffn_h2_s': _L0_ffn_in['h2_s'], 'L0_ffn_w3_w': _L0_ffn_in['w3_w'], 'L0_ffn_w3_s': _L0_ffn_in['w3_s']}
    _x0 = _d['L0_attn_hidden_states']
    _d['L0_attn_hidden_states'] = jax.random.normal(jax.random.fold_in(jax.random.key(seed), 1), (8, 1024, 128), dtype=_x0.dtype)
    del _x0
    return _d

def reference(L0_attn_hidden_states, L0_attn_W_basis, L0_attn_W_v, L0_attn_b_v, L0_attn_W_o, L0_attn_b_o, L0_ffn_w1_w, L0_ffn_w1_s, L0_ffn_w2_w, L0_ffn_w2_s, L0_ffn_h1_w, L0_ffn_h1_s, L0_ffn_h2_w, L0_ffn_h2_s, L0_ffn_w3_w, L0_ffn_w3_s):

    def _L0_attn_ref(hidden_states, W_basis, W_v, b_v, W_o, b_o):
        import math
        import jax, jax.numpy as jnp
        import numpy as np
        N_HEAD = 16
        B, T, C = hidden_states.shape
        nh = N_HEAD
        hd = C // nh
        R = W_basis.shape[0]
        latent = hidden_states @ W_basis.T
        v = hidden_states @ W_v.T + b_v
        v = v.reshape(B, T, nh, hd).transpose(0, 2, 1, 3)
        scores = jnp.einsum('bqr,bkr->bqk', latent, latent) * (1.0 / math.sqrt(R))
        causal = jnp.tril(jnp.ones((T, T), dtype=bool))
        scores = jnp.where(causal[None, :, :], scores, -jnp.inf)
        att = jax.nn.softmax(scores, axis=-1)
        y = jnp.einsum('bqk,bhkd->bhqd', att, v)
        y = y.transpose(0, 2, 1, 3).reshape(B, T, C)
        out = y @ W_o.T + b_o
        return out

    def _L0_ffn_ref(x, w1_w, w1_s, w2_w, w2_s, h1_w, h1_s, h2_w, h2_s, w3_w, w3_s):
        import jax, jax.numpy as jnp
        import numpy as np
        D_IN, D_HID = (128, 512)

        def _ternary(key, shape):
            return jax.random.randint(key, shape, -1, 2).astype(jnp.float32)

        def _tlin(x, w, s):
            return jnp.einsum('bsi,oi->bso', x, w) * s
        h = jax.nn.silu(_tlin(x, w1_w, w1_s)) * _tlin(x, w2_w, w2_s)
        h = jax.nn.gelu(_tlin(h, h1_w, h1_s), approximate=False)
        h = jax.nn.gelu(_tlin(h, h2_w, h2_s), approximate=False)
        return _tlin(h, w3_w, w3_s)
    x = L0_attn_hidden_states
    x = x + _layernorm(_L0_attn_ref(_layernorm(x, axis=-1), L0_attn_W_basis, L0_attn_W_v, L0_attn_b_v, L0_attn_W_o, L0_attn_b_o), axis=-1)
    x = x + _layernorm(_L0_ffn_ref(_layernorm(x, axis=-1), L0_ffn_w1_w, L0_ffn_w1_s, L0_ffn_w2_w, L0_ffn_w2_s, L0_ffn_h1_w, L0_ffn_h1_s, L0_ffn_h2_w, L0_ffn_h2_s, L0_ffn_w3_w, L0_ffn_w3_s), axis=-1)
    return x

_drawn_inputs = setup_inputs


def setup_inputs(seed=0):
    import zlib

    import numpy as np

    out = dict(_drawn_inputs(seed))
    spreads = {'L0_attn_b_v': (0.0, 0.1), 'L0_attn_b_o': (0.0, 0.1)}
    factors = {}
    for name, (base, spread) in spreads.items():
        noise = np.random.default_rng([zlib.crc32(name.encode()), seed]).standard_normal(out[name].shape)
        drawn = base * np.exp(spread * noise) if base else spread * noise
        out[name] = jnp.asarray(drawn.astype(out[name].dtype))
    for name, factor in factors.items():
        out[name] = (out[name] * factor).astype(out[name].dtype)
    return out
```

```python
from contextlib import ExitStack

import concourse.bass as bass
from concourse import mybir

F32 = mybir.dt.float32
F32R = mybir.dt.float32r
BF16 = mybir.dt.bfloat16
I32 = mybir.dt.int32
U32 = mybir.dt.uint32
ALU = mybir.AluOpType
ACT = mybir.ActivationFunctionType
AX_X = mybir.AxisListType.X

P = 128
BANK = 512
EPS = 1e-5
NEG = -3.0e38
RSQRT_SEED = 0x5F3759DF
NEWTON = 3


def layer_kernel(nc, x, w_basis_dup_t, w_v, w_o_t, b_v, b_o, w_up_t, s_up, w_down_t, s_down, out):
    T = x.shape[1]
    B = x.shape[0]
    C = x.shape[2]
    R = w_basis_dup_t.shape[1] // 2
    FC = w_up_t.shape[0] // P - 1
    HID = w_up_t.shape[1]
    KC = HID // P
    NT = T // P
    HALVES = T // BANK
    G = B * T // BANK
    GT = BANK // P
    SCALE = float(R) ** -0.5
    assert C == P and 2 * R == P and HALVES == 2 and FC + 1 == 2 + 2 * KC and B % 2 == 0

    chunks = [(j, q, min(BANK, T - q)) for j in range(NT) for q in range(j * P, T, BANK)]
    NCH = len(chunks)
    chunks_to = [sum(c[0] <= j for c in chunks) for j in range(NT)]
    probs_at = [sum(T - i * P for i in range(j)) for j in range(NT)]
    probs_cols = sum(T - j * P for j in range(NT))
    max_order = list(reversed(range(NT)))

    with ExitStack() as ctx:
        def sb(name, shape, dt=F32, scope=ctx):
            return scope.enter_context(nc.sbuf_tensor(name, shape, dt))

        def sem(name):
            return ctx.enter_context(nc.semaphore(name))

        x_sb = sb("x_sb", [P, B * NT, C])
        w_hi = sb("w_hi", [P, 2 + 2 * KC, HID], F32R)
        w_lo = sb("w_lo", [P, 2 + 2 * KC, HID], F32R)
        w_down = sb("w_down", [P, KC, C])
        scales = sb("scales", [P, 4, KC])
        s_down_bc = sb("s_down_bc", [P, C])
        ident = sb("ident", [P, P])
        ident_bf = sb("ident_bf", [P, P], BF16)
        mask_q = sb("mask_q", [P, P], BF16)
        mask_k = sb("mask_k", [P, P], BF16)
        ones = sb("ones", [P, 2])
        lo_max = sb("lo_max", [P, 1])
        lo_flag = sb("lo_flag", [1, 1], I32)
        bn = sb("bn", [P, NT, 6])
        ln_mean = sb("ln_mean", [P, NT])
        ln_var = sb("ln_var", [P, NT])
        ln1_y = sb("ln1_y", [P, NT])
        ln_t = sb("ln_t", [P, NT])
        ln1_nb = sb("ln1_nb", [P, NT])
        post_bn = sb("post_bn", [P, NT, 6])
        post_mean = sb("post_mean", [P, NT])
        post_v2 = sb("post_v2", [P, NT])
        post_v = sb("post_v", [P, NT])
        post_y = sb("post_y", [P, NT])
        post_t = sb("post_t", [P, NT])

        with ExitStack() as one:
            w_raw = sb("w_raw", [P, 2 + 2 * KC, HID], F32, one)
            w_basis = sb("w_basis", [P, P], F32, one)
            w_v_sb = sb("w_v_sb", [P, P], F32, one)
            w_o_sb = sb("w_o_sb", [P, P], F32, one)
            w_vo = sb("w_vo", [P, P], F32, one)
            b_v_col = sb("b_v_col", [P, 1], F32, one)
            b_v_bc = sb("b_v_bc", [P, P], F32, one)
            b_o_bc = sb("b_o_bc", [P, P], F32, one)
            b_vo_bc = sb("b_vo_bc", [P, P], F32, one)
            xn = sb("xn", [P, NT, C], F32, one)
            xt = sb("xt", [P, T], F32, one)
            lat_hh = [sb(f"lat_hh{p}", [P, T], F32R, one) for p in range(2)]
            lat_hl = [sb(f"lat_hl{p}", [P, T], F32R, one) for p in range(2)]
            lat_l1 = [sb(f"lat_l1{p}", [R + 1, T], F32R, one) for p in range(2)]
            lat_hm = [sb(f"lat_hm{p}", [R + 1, T], F32R, one) for p in range(2)]
            values = [sb(f"values{p}", [P, NT, C + 1], F32, one) for p in range(2)]
            probs = sb("probs", [P, probs_cols], F32, one)
            row_max = sb("row_max", [P, NT], F32, one)
            o_sb = [sb(f"o_sb{p}", [P, NT, C + 1], F32, one) for p in range(2)]
            o_ln = sb("o_ln", [P, NT, C], F32, one)
        with ExitStack() as two:
            xn2 = sb("xn2", [P, GT, C], F32, two)
            xt_hi = sb("xt_hi", [P, BANK], F32R, two)
            xt_lo = sb("xt_lo", [P, BANK], F32R, two)
            gate = sb("gate", [P, 2, BANK], F32, two)
            h1_full = sb("h1_full", [P, 2, BANK], F32, two)
            h2_full = sb("h2_full", [P, 2, BANK], F32, two)
            h1_hi = sb("h1_hi", [P, KC, BANK], F32R, two)
            h1_lo = sb("h1_lo", [P, KC, BANK], F32R, two)
            h2_hi = sb("h2_hi", [P, KC, BANK], F32R, two)
            h2_lo = sb("h2_lo", [P, KC, BANK], F32R, two)
            h3 = sb("h3", [P, KC, BANK], F32, two)
            y = sb("y", [P, GT, C], F32, two)
            y_ln = sb("y_ln", [P, GT, C], F32, two)

        with ExitStack() as one:
            ps = lambda name, shape: one.enter_context(nc.psum_tensor(name, shape, F32))
            ps_prep = ps("ps_prep", [P, 2, BANK])
            ps_max = ps("ps_max", [P, 2, BANK])
            ps_s = ps("ps_s", [P, 2, BANK])
            ps_o = ps("ps_o", [P, 2, BANK])
        with ExitStack() as two:
            ps = lambda name, shape: two.enter_context(nc.psum_tensor(name, shape, F32))
            ps_g = ps("ps_g", [P, 2, BANK])
            ps_u = ps("ps_u", [P, 2, BANK])
            ps_h = ps("ps_h", [P, 2, BANK])
            ps_t = ps("ps_t", [P, GT, P])
            ps_y = ps("ps_y", [P, GT, C])

        consts_ready = sem("consts_ready")
        w_attn_loaded = sem("w_attn_loaded")
        w_mlp_loaded = sem("w_mlp_loaded")
        x_loaded = sem("x_loaded")
        out_stored = sem("out_stored")
        setup_pe = sem("setup_pe")
        setup_dve = sem("setup_dve")
        pool_step = sem("pool_step")
        w_split = sem("w_split")
        flag_step = sem("flag_step")
        ln1_step = sem("ln1_step")
        xn_ready = sem("xn_ready")
        t_done = sem("t_done")
        xt_ready = sem("xt_ready")
        lat_done = sem("lat_done")
        hi_ready = sem("hi_ready")
        hi_copied = sem("hi_copied")
        lo_ready = sem("lo_ready")
        val_done = sem("val_done")
        val_ready = sem("val_ready")
        max_scores_done = sem("max_scores_done")
        max_ready = sem("max_ready")
        max_row_done = sem("max_row_done")
        max_row_ready = sem("max_row_ready")
        scores_done = sem("scores_done")
        probs_ready = sem("probs_ready")
        o_done = sem("o_done")
        o_ready = sem("o_ready")
        post_step = sem("post_step")
        o_ln_ready = sem("o_ln_ready")
        x1_ready = sem("x1_ready")
        ln2_step = sem("ln2_step")
        xn2_ready = sem("xn2_ready")
        t2_done = sem("t2_done")
        xt2_ready = sem("xt2_ready")
        up_done = sem("up_done")
        gate_ready = sem("gate_ready")
        gated = sem("gated")
        h1_ready = sem("h1_ready")
        h2_done = sem("h2_done")
        h2_act = sem("h2_act")
        h2_hi_ready = sem("h2_hi_ready")
        h2_ready = sem("h2_ready")
        h3_done = sem("h3_done")
        h3_ready = sem("h3_ready")
        y_done = sem("y_done")
        y_read = sem("y_read")
        fin_step = sem("fin_step")
        y_ln_ready = sem("y_ln_ready")
        out_ready = sem("out_ready")

        class Steps:

            def __init__(self, eng, semaphore, base):
                self.eng, self.sem, self.value = eng, semaphore, base

            def then(self, ins):
                ins.then_inc(self.sem, 1)
                self.value = self.value + 1
                self.eng.wait_ge(self.sem, self.value)

        AGGREGATE_STEPS = 5

        def aggregate(v, steps, stats, mean, var, d, eps):
            n = C // 2
            steps.then(v.tensor_tensor(d, stats[:, :, 1], stats[:, :, 4], ALU.subtract))
            steps.then(v.tensor_tensor(mean, stats[:, :, 1], stats[:, :, 4], ALU.add))
            v.tensor_scalar(mean, mean, 0.5, None, ALU.mult)
            steps.then(v.scalar_tensor_tensor(out=d, in0=d, scalar=0.25, in1=d, op0=ALU.mult, op1=ALU.mult))
            steps.then(v.scalar_tensor_tensor(out=var, in0=stats[:, :, 2], scalar=2 * n * eps,
                                              in1=stats[:, :, 5], op0=ALU.add, op1=ALU.add))
            steps.then(v.scalar_tensor_tensor(out=var, in0=var, scalar=0.5 / n, in1=d,
                                              op0=ALU.mult, op1=ALU.add))

        RSQRT_STEPS = 1 + 3 * NEWTON

        def rsqrt(v, steps, y_, t_, var):
            steps.then(v.tensor_scalar(y_.bitcast(I32), var.bitcast(I32), -0.5, float(RSQRT_SEED),
                                       ALU.mult, ALU.add))
            for _ in range(NEWTON):
                steps.then(v.scalar_tensor_tensor(out=t_, in0=y_, scalar=-0.5, in1=y_,
                                                  op0=ALU.mult, op1=ALU.mult))
                steps.then(v.tensor_tensor(t_, t_, var, ALU.mult))
                steps.then(v.scalar_tensor_tensor(out=y_, in0=t_, scalar=1.5, in1=y_,
                                                  op0=ALU.add, op1=ALU.mult))

        LN1_STEPS = 2 + AGGREGATE_STEPS + RSQRT_STEPS + 1
        POST_STEPS = 1 + AGGREGATE_STEPS + 2 + RSQRT_STEPS
        LN2_STEPS = 1 + AGGREGATE_STEPS + RSQRT_STEPS
        FIN_STEPS = 1 + AGGREGATE_STEPS + RSQRT_STEPS

        block = ctx.enter_context(nc.Block())

        @block.sync
        def _(sp):
            xr = x.rearrange("b (t p) c -> b p t c", p=P)

            def load_x(b, b_dram):
                sp.dma_start(x_sb[:, bass.ts(b, NT), :], xr[b_dram]).then_inc(x_loaded, 16)

            load_x(0, 0)
            for dst, src in ((w_basis[:], w_basis_dup_t), (w_v_sb[:], w_v), (w_o_sb[:], w_o_t),
                             (b_v_col[:], b_v), (b_o_bc[:], b_o.to_broadcast([P, C]))):
                sp.dma_start(dst, src).then_inc(w_attn_loaded, 16)
            for b in range(1, B):
                sp.wait_ge(x_loaded, 16 * b)
                load_x(b, b)
            for dst, src in ((w_raw[:], w_up_t.rearrange("(k p) n -> p k n", p=P)),
                             (w_down[:], w_down_t.rearrange("(k p) n -> p k n", p=P)),
                             (scales[:], s_up), (s_down_bc[:], s_down.to_broadcast([P, C]))):
                sp.dma_start(dst, src).then_inc(w_mlp_loaded, 16)
            outr = out.rearrange("b (h t p) c -> (b h) p t c", p=P, t=GT)
            with sp.Fori(0, G) as g:
                sp.wait_ge(out_ready, g + 1)
                sp.dma_start(outr[bass.ds(g, 1)].rearrange("g p t c -> (g p) t c"),
                             x_sb[:, bass.ts(g, GT), :]).then_inc(out_stored, 16)
            sp.wait_ge(out_stored, 16 * G)

        @block.gpsimd
        def _(pool):
            st = Steps(pool, pool_step, 0)
            st.then(pool.memset(ident[:], 0.0))
            st.then(pool.affine_select(out=ident[:], in_=ident[:], compare_op=ALU.not_equal, fill=1.0,
                                       base=0, pattern=[[-1, P]], channel_multiplier=1))
            st.then(pool.tensor_copy(ident_bf[:], ident[:]))
            st.then(pool.memset(mask_q[:], 0.0))
            st.then(pool.affine_select(out=mask_q[:], in_=mask_q[:], compare_op=ALU.is_ge, fill=NEG,
                                       base=0, pattern=[[-1, P]], channel_multiplier=1))
            st.then(pool.memset(mask_k[:], 0.0))
            st.then(pool.affine_select(out=mask_k[:], in_=mask_k[:], compare_op=ALU.is_ge, fill=NEG,
                                       base=0, pattern=[[1, P]], channel_multiplier=-1))
            st.then(pool.memset(ones[:], 1.0))
            for p in range(2):
                st.then(pool.memset(values[p][:, :, C:C + 1], 1.0))
                st.then(pool.memset(lat_l1[p][R:R + 1, :].bitcast(F32), 1.0))
            pool.memset(lo_max[:], 0.0).then_inc(consts_ready, 1)

            def copy_hi(b, p):
                for h in range(HALVES):
                    s = slice(h * BANK, (h + 1) * BANK)
                    pool.wait_ge(hi_ready, HALVES * b + h + 1)
                    pool.tensor_tensor(lat_hl[p][0:R, s], lat_hh[p][0:R, s].bitcast(F32),
                                       ones[0:R, 0:1].to_broadcast([R, BANK]), ALU.mult)
                    pool.tensor_scalar(lat_hm[p][0:R, s], lat_hh[p][0:R, s].bitcast(F32), 1.0, 1.0,
                                       ALU.mult, ALU.mult).then_inc(hi_copied, 1)

            def add_x1(b):
                pool.wait_ge(o_ln_ready, b + 1)
                xs = x_sb[:, bass.ts(b, NT), :]
                pool.tensor_tensor(xs, xs, o_ln[:], ALU.add).then_inc(x1_ready, 1)

            copy_hi(0, 0)
            with pool.Fori(0, B // 2 - 1) as i:
                for p in range(2):
                    copy_hi(2 * i + p + 1, 1 - p)
                    add_x1(2 * i + p)
            copy_hi(B - 1, 1)
            pool.wait_ge(w_mlp_loaded, 64)
            for k in range(2 + 2 * KC):
                pool.tensor_scalar(w_hi[:, k], w_raw[:, k], 1.0, 1.0, ALU.mult,
                                   ALU.mult).then_inc(w_split, 1)
            add_x1(B - 2)
            for k in range(2 + 2 * KC):
                pool.wait_ge(w_split, 2 + 2 * KC + k)
                pool.tensor_tensor(w_lo[:, k], w_raw[:, k], w_hi[:, k].bitcast(F32),
                                   ALU.subtract).then_inc(w_split, 1)
            add_x1(B - 1)
            with pool.Fori(0, G) as g:
                pool.wait_ge(y_ln_ready, g + 1)
                xs = x_sb[:, bass.ts(g, GT), :]
                pool.tensor_tensor(xs, xs, y_ln[:], ALU.add).then_inc(out_ready, 1)

        @block.scalar
        def _(act):
            def normalise(b):
                act.wait_ge(ln1_step, LN1_STEPS * (b + 1))
                for t in range(NT):
                    ins = act.activation(xn[:, t, :], x_sb[:, bass.ds(b * NT + t, 1), :],
                                         ACT.Identity, bias=ln1_nb[:, t:t + 1], scale=ln1_y[:, t:t + 1])
                ins.then_inc(xn_ready, 1)

            def copy_xt(b):
                for h in range(HALVES):
                    act.wait_ge(t_done, HALVES * b + h + 1)
                    act.copy(xt[:, h * BANK:(h + 1) * BANK], ps_prep[:, h, :]).then_inc(xt_ready, 1)

            def round_lat(b, p):
                for h in range(HALVES):
                    act.wait_ge(lat_done, HALVES * b + h + 1)
                    act.copy(lat_hh[p][:, h * BANK:(h + 1) * BANK], ps_prep[:, h, :]).then_inc(hi_ready, 1)

            def exp(b, j):
                for n, (jj, q, width) in enumerate(chunks):
                    if jj == j:
                        act.wait_ge(scores_done, NCH * b + n + 1)
                        at = probs_at[j] + q - j * P
                        act.activation(probs[:, at:at + width], ps_s[:, n % 2, 0:width], ACT.Exp,
                                       scale=SCALE).then_inc(probs_ready, 1)

            def copy_o(b, p, t):
                act.wait_ge(o_done, NT * b + t + 1)
                act.copy(o_sb[p][:, t, :], ps_o[:, t % 2, 0:C + 1]).then_inc(o_ready, 1)

            def copy_max_row(b, p):
                for h in range(HALVES):
                    act.wait_ge(max_row_done, HALVES * b + h + 1)
                    act.mul(lat_hm[p][R:R + 1, h * BANK:(h + 1) * BANK], ps_prep[R:R + 1, h, :],
                            -1.0).then_inc(max_row_ready, 1)

            def step(b, p, prep, norm):
                if prep:
                    copy_xt(b + 1)
                exp(b, 0)
                if prep:
                    round_lat(b + 1, 1 - p)
                exp(b, 1)
                exp(b, 2)
                for t in range(NT):
                    copy_o(b, p, t)
                    if t + 3 < NT:
                        exp(b, t + 3)
                    if t == NT - 4 and norm:
                        normalise(b + 2)
                if prep:
                    copy_max_row(b + 1, 1 - p)

            normalise(0)
            copy_xt(0)
            round_lat(0, 0)
            normalise(1)
            copy_max_row(0, 0)
            with act.Fori(0, B // 2 - 1) as i:
                for p in range(2):
                    step(2 * i + p, p, True, True)
            step(B - 2, 0, True, False)
            step(B - 1, 1, False, False)

            def silu(g):
                for c in range(KC):
                    act.wait_ge(up_done, KC * g + c + 1)
                    act.activation(gate[:, c % 2, :], ps_g[:, c % 2, :], ACT.Silu,
                                   scale=scales[:, 0, c:c + 1]).then_inc(gate_ready, 1)

            def gelu2(g):
                for c in range(KC):
                    act.wait_ge(h2_done, KC * g + c + 1)
                    if c >= 2:
                        act.wait_ge(h2_ready, KC * g + c - 1)
                    act.activation(h2_full[:, c % 2, :], ps_h[:, c % 2, :], ACT.Gelu,
                                   scale=scales[:, 2, c:c + 1]).then_inc(h2_act, 1)

            def gelu3(g):
                for c in range(KC):
                    act.wait_ge(h3_done, KC * g + c + 1)
                    act.activation(h3[:, c, :], ps_h[:, c % 2, :], ACT.Gelu,
                                   scale=scales[:, 3, c:c + 1]).then_inc(h3_ready, 1)

            act.wait_ge(w_mlp_loaded, 64)
            silu(0)
            gelu2(0)
            with act.Fori(1, G) as g:
                silu(g)
                gelu3(g - 1)
                gelu2(g)
            gelu3(G - 1)

        @block.vector
        def _(v):
            def setup():
                v.wait_ge(w_attn_loaded, 80)
                v.tensor_copy(b_v_bc[:], b_v_col[:].to_broadcast([P, P])).then_inc(setup_dve, 1)
                v.wait_ge(setup_pe, 1)
                v.tensor_copy(w_vo[:], ps_prep[:, 0, 0:P]).then_inc(setup_dve, 1)
                v.wait_ge(setup_pe, 2)
                v.tensor_tensor(b_vo_bc[:], ps_prep[:, 1, 0:P], b_o_bc[:], ALU.add).then_inc(setup_dve, 1)

            def ln1_stats(b, tiles):
                if tiles[0] == 0:
                    v.wait_ge(x_loaded, 16 * (b + 1))
                for t in tiles:
                    ins = v.bn_stats(bn[:, t, :], x_sb[:, bass.ds(b * NT + t, 1), :])
                ins.then_inc(ln1_step, 1)

            def ln1_scale(b):
                v.wait_ge(ln1_step, LN1_STEPS * b + 2)
                st = Steps(v, ln1_step, LN1_STEPS * b + 2)
                aggregate(v, st, bn[:], ln_mean[:], ln_var[:], ln_t[:], EPS)
                return st

            def lo_lat(b, p):
                for h in range(HALVES):
                    s = slice(h * BANK, (h + 1) * BANK)
                    v.wait_ge(hi_ready, HALVES * b + h + 1)
                    v.tensor_tensor(lat_hl[p][R:P, s], ps_prep[R:P, h, :],
                                    lat_hh[p][R:P, s].bitcast(F32), ALU.subtract)
                    v.tensor_tensor(lat_l1[p][0:R, s], ps_prep[0:R, h, :],
                                    lat_hh[p][0:R, s].bitcast(F32), ALU.subtract).then_inc(lo_ready, 1)

            def bias_values(b, p):
                for h in range(HALVES):
                    v.wait_ge(val_done, HALVES * b + h + 1)
                    n = BANK // P
                    v.tensor_tensor(values[p][:, h * n:(h + 1) * n, 0:C],
                                    ps_prep[:, h, :].rearrange("p (t c) -> p t c", c=C),
                                    b_vo_bc[:].unsqueeze(1).to_broadcast([P, n, C]),
                                    ALU.add).then_inc(val_ready, 1)

            def take_max(b, n):
                t = max_order[n]
                v.wait_ge(max_scores_done, NT * b + n + 1)
                v.reduce_max(row_max[:, t:t + 1], ps_max[:].rearrange("p b n -> p (b n)")[:, 0:(t + 1) * P],
                             AX_X).then_inc(max_ready, 1)

            def post(b, p, last):
                st = Steps(v, post_step, POST_STEPS * b)
                for t in range(NT):
                    v.wait_ge(o_ready, NT * b + t + 1)
                    ins = v.bn_stats(post_bn[:, t, :], o_sb[p][:, t, 0:C])
                st.then(ins)
                aggregate(v, st, post_bn[:], post_mean[:], post_v2[:], post_t[:], 0.0)
                r = o_sb[p][:, :, C]
                st.then(v.scalar_tensor_tensor(out=post_v[:], in0=r, scalar=EPS, in1=r,
                                               op0=ALU.mult, op1=ALU.mult))
                st.then(v.tensor_tensor(post_v[:], post_v[:], post_v2[:], ALU.add))
                rsqrt(v, st, post_y[:], post_t[:], post_v[:])
                if last:
                    v.wait_ge(x1_ready, b)
                for t in range(NT):
                    ins = v.tensor_scalar(o_ln[:, t, :], o_sb[p][:, t, 0:C], post_mean[:, t:t + 1],
                                          post_y[:, t:t + 1], ALU.subtract, ALU.mult)
                ins.then_inc(o_ln_ready, 1)

            def ln1_finish(st):
                rsqrt(v, st, ln1_y[:], ln_t[:], ln_var[:])
                st.then(v.scalar_tensor_tensor(out=ln1_nb[:], in0=ln_mean[:], scalar=-1.0,
                                               in1=ln1_y[:], op0=ALU.mult, op1=ALU.mult))

            half_tiles = [list(range(NT // 2)), list(range(NT // 2, NT))]

            def step(b, p, prep, norm):
                if prep:
                    lo_lat(b + 1, 1 - p)
                    bias_values(b + 1, 1 - p)
                    for n in range(NT):
                        take_max(b + 1, n)
                        if norm and n < 2:
                            ln1_stats(b + 2, half_tiles[n])
                        if norm and n == 2:
                            st = ln1_scale(b + 2)
                        if norm and n == 3:
                            ln1_finish(st)
                post(b, p, not prep)

            for b in range(2):
                for h in range(2):
                    ln1_stats(b, half_tiles[h])
                if b:
                    v.wait_ge(xn_ready, b)
                ln1_finish(ln1_scale(b))
                if b == 0:
                    setup()
            lo_lat(0, 0)
            bias_values(0, 0)
            for n in range(NT):
                take_max(0, n)
            with v.Fori(0, B // 2 - 1) as i:
                for p in range(2):
                    step(2 * i + p, p, True, True)
            step(B - 2, 0, True, False)
            step(B - 1, 1, False, False)

            v.wait_ge(w_split, 2 * (2 + 2 * KC))
            v.tensor_reduce(lo_max[:], w_lo[:].rearrange("p k n -> p (k n)").bitcast(U32), AX_X,
                            ALU.max).then_inc(flag_step, 1)
            v.wait_ge(flag_step, 2)
            v.tensor_scalar(lo_flag[:], ps_o[0:1, 0, 0:1], 0.0, None, ALU.is_gt).then_inc(flag_step, 1)

            def ln2(g):
                st = Steps(v, ln2_step, LN2_STEPS * g)
                for t in range(GT):
                    ins = v.bn_stats(bn[:, t, :], x_sb[:, bass.ds(g * GT + t, 1), :])
                st.then(ins)
                aggregate(v, st, bn[:, 0:GT], ln_mean[:, 0:GT], ln_var[:, 0:GT], ln_t[:, 0:GT], EPS)
                rsqrt(v, st, ln1_y[:, 0:GT], ln_t[:, 0:GT], ln_var[:, 0:GT])
                for t in range(GT):
                    ins = v.tensor_scalar(xn2[:, t, :], x_sb[:, bass.ds(g * GT + t, 1), :],
                                          ln_mean[:, t:t + 1], ln1_y[:, t:t + 1], ALU.subtract, ALU.mult)
                ins.then_inc(xn2_ready, 1)

            def split_xt(g):
                v.wait_ge(t2_done, g + 1)
                pt = ps_t[:].rearrange("p t c -> p (t c)")
                v.tensor_copy(xt_hi[:], pt).then_inc(xt2_ready, 1)
                v.wait_ge(xt2_ready, 2 * g + 1)
                v.tensor_tensor(xt_lo[:], pt, xt_hi[:].bitcast(F32), ALU.subtract).then_inc(xt2_ready, 1)

            def gate_h1(g):
                for c in range(KC):
                    v.wait_ge(gate_ready, KC * g + c + 1)
                    v.scalar_tensor_tensor(out=h1_full[:, c % 2, :], in0=ps_u[:, c % 2, :],
                                           scalar=scales[:, 1, c:c + 1], in1=gate[:, c % 2, :],
                                           op0=ALU.mult, op1=ALU.mult).then_inc(gated, 1)
                    v.wait_ge(gated, KC * g + c + 1)
                    v.tensor_copy(h1_hi[:, c, :], h1_full[:, c % 2, :]).then_inc(h1_ready, 1)
                    v.wait_ge(h1_ready, 2 * (KC * g + c) + 1)
                    v.tensor_tensor(h1_lo[:, c, :], h1_full[:, c % 2, :], h1_hi[:, c, :].bitcast(F32),
                                    ALU.subtract).then_inc(h1_ready, 1)

            def split_h2(g):
                for c in range(KC):
                    v.wait_ge(h2_act, KC * g + c + 1)
                    v.tensor_copy(h2_hi[:, c, :], h2_full[:, c % 2, :]).then_inc(h2_hi_ready, 1)
                    v.wait_ge(h2_hi_ready, KC * g + c + 1)
                    v.tensor_tensor(h2_lo[:, c, :], h2_full[:, c % 2, :], h2_hi[:, c, :].bitcast(F32),
                                    ALU.subtract).then_inc(h2_ready, 1)

            def finish(g, first=False):
                v.wait_ge(y_done, g + 1)
                st = Steps(v, fin_step, FIN_STEPS * g)
                if not first:
                    v.wait_ge(y_ln_ready, g)
                v.tensor_tensor(y[:], ps_y[:], s_down_bc[:].unsqueeze(1).to_broadcast([P, GT, C]),
                                ALU.mult).then_inc(y_read, 1)
                v.wait_ge(y_read, g + 1)
                for t in range(GT):
                    ins = v.bn_stats(post_bn[:, t, :], y[:, t, :])
                st.then(ins)
                aggregate(v, st, post_bn[:, 0:GT], post_mean[:, 0:GT], post_v[:, 0:GT], post_t[:, 0:GT], EPS)
                rsqrt(v, st, post_y[:, 0:GT], post_t[:, 0:GT], post_v[:, 0:GT])
                if not first:
                    v.wait_ge(out_ready, g)
                for t in range(GT):
                    ins = v.tensor_scalar(y_ln[:, t, :], y[:, t, :], post_mean[:, t:t + 1],
                                          post_y[:, t:t + 1], ALU.subtract, ALU.mult)
                ins.then_inc(y_ln_ready, 1)

            v.wait_ge(w_mlp_loaded, 64)
            v.wait_ge(x1_ready, B)
            ln2(0)
            split_xt(0)
            for g in range(3):
                gate_h1(g)
                ln2(g + 1)
                if g == 2:
                    finish(0, True)
                split_xt(g + 1)
                split_h2(g)
            with v.Fori(3, G - 1) as g:
                gate_h1(g)
                ln2(g + 1)
                finish(g - 2)
                split_xt(g + 1)
                split_h2(g)
            gate_h1(G - 1)
            finish(G - 3)
            split_h2(G - 1)
            finish(G - 2)
            finish(G - 1)

        @block.tensor
        def _(pe):
            pe.wait_ge(consts_ready, 1)
            pe.wait_ge(w_attn_loaded, 80)
            pe.matmul(ps_prep[:, 0, 0:P], w_v_sb[:], w_o_sb[:], start=True, stop=True).then_inc(setup_pe, 1)
            pe.wait_ge(setup_dve, 1)
            pe.matmul(ps_prep[:, 1, 0:P], b_v_bc[:], w_o_sb[:], start=True, stop=True).then_inc(setup_pe, 1)
            pe.wait_ge(setup_dve, 3)

            def transpose_x(b, first=False):
                pe.wait_ge(xn_ready, b + 1)
                if not first:
                    pe.wait_ge(max_row_ready, HALVES * b)
                for t in range(NT):
                    h, c = divmod(t * P, BANK)
                    ins = pe.transpose(ps_prep[:, h, c:c + P], xn[:, t, :], ident[:])
                    if c + P == BANK:
                        ins.then_inc(t_done, 1)

            def latents(b):
                for h in range(HALVES):
                    pe.wait_ge(xt_ready, HALVES * b + h + 1)
                    pe.matmul(ps_prep[:, h, :], w_basis[:], xt[:, h * BANK:(h + 1) * BANK],
                              start=True, stop=True).then_inc(lat_done, 1)

            def make_values(b):
                pe.wait_ge(lo_ready, HALVES * (b + 1))
                for t in range(NT):
                    h, c = divmod(t * P, BANK)
                    ins = pe.matmul(ps_prep[:, h, c:c + P], xt[:, t * P:(t + 1) * P], w_vo[:],
                                    start=True, stop=True)
                    if c + P == BANK:
                        ins.then_inc(val_done, 1)

            def max_scores(b, p, n, first=False):
                t = max_order[n]
                if n == 0:
                    pe.wait_ge(hi_copied, HALVES * (b + 1))
                    pe.wait_ge(lo_ready, HALVES * (b + 1))
                if not (first and n == 0):
                    pe.wait_ge(max_ready, NT * b + n)
                end = (t + 1) * P
                for k in range(0, end, BANK):
                    width = min(BANK, end - k)
                    pe.matmul(ps_max[:, k // BANK, 0:width], lat_hh[p][:, t * P:end],
                              lat_hl[p][:, k:k + width], start=True, stop=k + width < end)
                h, c = divmod(t * P, BANK)
                pe.matmul(ps_max[:, h, c:c + P], ident_bf[:], mask_q[:], start=False,
                          stop=True).then_inc(max_scores_done, 1)

            def lay_max(b):
                pe.wait_ge(max_ready, NT * (b + 1))
                pe.wait_ge(val_ready, HALVES * (b + 1))
                for t in range(NT):
                    h, c = divmod(t * P, BANK)
                    ins = pe.matmul(ps_prep[R:R + 1, h, c:c + P], row_max[:, t:t + 1], ident[:],
                                    start=True, stop=True)
                    if c + P == BANK:
                        ins.then_inc(max_row_done, 1)

            def scores(b, p, j):
                if j == 0:
                    pe.wait_ge(max_row_ready, HALVES * (b + 1))
                for n, (jj, q, width) in enumerate(chunks):
                    if jj != j:
                        continue
                    if n >= 2:
                        pe.wait_ge(probs_ready, NCH * b + n - 1)
                    own = q == j * P
                    k = slice(j * P, (j + 1) * P)
                    pe.matmul(ps_s[:, n % 2, 0:width], lat_hh[p][:, k], lat_hl[p][:, q:q + width],
                              start=True, stop=False)
                    ins = pe.matmul(ps_s[:, n % 2, 0:width], lat_l1[p][:, k], lat_hm[p][:, q:q + width],
                                    start=False, stop=not own)
                    if own:
                        ins = pe.matmul(ps_s[:, n % 2, 0:P], ident_bf[:], mask_k[:], start=False, stop=True)
                    ins.then_inc(scores_done, 1)

            def attend(b, p, t):
                pe.wait_ge(probs_ready, NCH * b + chunks_to[t])
                if t >= 2:
                    pe.wait_ge(o_ready, NT * b + t - 1)
                for j in range(t + 1):
                    at = probs_at[j] + (t - j) * P
                    ins = pe.matmul(ps_o[:, t % 2, 0:C + 1], probs[:, at:at + P], values[p][:, j, :],
                                    start=(j == 0), stop=(j == t))
                ins.then_inc(o_done, 1)

            def step(b, p, prep):
                if prep:
                    transpose_x(b + 1)
                scores(b, p, 0)
                if prep:
                    latents(b + 1)
                scores(b, p, 1)
                attend(b, p, 0)
                scores(b, p, 2)
                attend(b, p, 1)
                scores(b, p, 3)
                if prep:
                    make_values(b + 1)
                attend(b, p, 2)
                scores(b, p, 4)
                turns = {3: (0,), 4: (1, 2), 5: (3, 4), 6: (5, 6), 7: (7,)}
                for t in range(3, NT):
                    for n in turns[t] if prep else ():
                        max_scores(b + 1, 1 - p, n)
                    attend(b, p, t)
                    if t + 2 < NT:
                        scores(b, p, t + 2)
                if prep:
                    lay_max(b + 1)

            transpose_x(0, True)
            latents(0)
            make_values(0)
            for n in range(NT):
                max_scores(0, 0, n, True)
            lay_max(0)
            with pe.Fori(0, B // 2 - 1) as i:
                for p in range(2):
                    step(2 * i + p, p, True)
            step(B - 2, 0, True)
            step(B - 1, 1, False)

            pe.wait_ge(flag_step, 1)
            pe.wait_ge(o_ready, NT * B)
            pe.matmul(ps_o[0:1, 0, 0:1], lo_max[:], ones[:, 0:1], start=True, stop=True).then_inc(flag_step, 1)
            pe.wait_ge(flag_step, 3)
            any_lo = pe.value_load(lo_flag[0:1, 0:1], min_val=0, max_val=1)

            def product(bank, k0, ks, c, hi, lo, general):
                cols = slice(c * P, (c + 1) * P)
                for k in range(ks):
                    passes = [(w_hi, hi), (w_hi, lo)] + ([(w_lo, hi)] if general else [])
                    for n, (w, h) in enumerate(passes):
                        ins = pe.matmul(bank, w[:, k0 + k, cols], h(k), start=(k == 0 and n == 0),
                                        stop=(k == ks - 1 and n == len(passes) - 1))
                return ins

            def transpose_x1(g):
                pe.wait_ge(xn2_ready, g + 1)
                for t in range(GT):
                    ins = pe.transpose(ps_t[:, t, :], xn2[:, t, :], ident[:])
                ins.then_inc(t2_done, 1)

            def up(g, general):
                pe.wait_ge(xt2_ready, 2 * (g + 1))
                for c in range(KC):
                    if c >= 2:
                        pe.wait_ge(gated, KC * g + c - 1)
                    product(ps_g[:, c % 2, :], 0, 1, c, lambda k: xt_hi[:], lambda k: xt_lo[:], general)
                    product(ps_u[:, c % 2, :], 1, 1, c, lambda k: xt_hi[:], lambda k: xt_lo[:],
                            general).then_inc(up_done, 1)

            def hidden2(g, general, first=False):
                pe.wait_ge(h1_ready, 2 * KC * (g + 1))
                for c in range(KC):
                    if c >= 2:
                        pe.wait_ge(h2_act, KC * g + c - 1)
                    elif not first:
                        pe.wait_ge(h3_ready, KC * g + c - 1)
                    product(ps_h[:, c % 2, :], 2, KC, c, lambda k: h1_hi[:, k, :],
                            lambda k: h1_lo[:, k, :], general).then_inc(h2_done, 1)

            def hidden3(g, general):
                pe.wait_ge(h2_ready, KC * (g + 1))
                for c in range(KC):
                    if c >= 2:
                        pe.wait_ge(h3_ready, KC * g + c - 1)
                    product(ps_h[:, c % 2, :], 2 + KC, KC, c, lambda k: h2_hi[:, k, :],
                            lambda k: h2_lo[:, k, :], general).then_inc(h3_done, 1)

            def down(g, first=False):
                pe.wait_ge(h3_ready, KC * (g + 1))
                if not first:
                    pe.wait_ge(y_read, g)
                for t in range(GT):
                    for k in range(KC):
                        ins = pe.matmul(ps_y[:, t, :], h3[:, k, t * P:(t + 1) * P], w_down[:, k, :],
                                        start=(k == 0), stop=(k == KC - 1))
                ins.then_inc(y_done, 1)

            def mlp(general):
                up(0, general)
                transpose_x1(1)
                hidden2(0, general, True)
                up(1, general)
                hidden3(0, general)
                transpose_x1(2)
                hidden2(1, general)
                down(0, True)
                with pe.Fori(2, G - 1) as g:
                    up(g, general)
                    hidden3(g - 1, general)
                    transpose_x1(g + 1)
                    hidden2(g, general)
                    down(g - 1)
                up(G - 1, general)
                hidden3(G - 2, general)
                hidden2(G - 1, general)
                down(G - 2)
                hidden3(G - 1, general)
                down(G - 1)

            transpose_x1(0)
            with pe.If(any_lo):
                mlp(True)
            with pe.Else():
                mlp(False)


def kernel(**inputs):
    import numpy as np
    import concourse.bacc as bacc
    from concourse import mybir as mb
    from concourse.bass_utils import run_bass_kernel_spmd

    def a(name):
        return np.asarray(inputs[name])

    hidden = a("L0_ffn_h1_w").shape[0]
    wb = a("L0_attn_W_basis").T
    in_map = {
        "x": a("L0_attn_hidden_states"),
        "w_basis_dup_t": np.concatenate([wb, wb], axis=1),
        "w_v": a("L0_attn_W_v"),
        "w_o_t": a("L0_attn_W_o").T,
        "b_v": a("L0_attn_b_v").reshape(-1, 1),
        "b_o": a("L0_attn_b_o").reshape(1, -1),
        "w_up_t": np.concatenate([a(f"L0_ffn_{n}_w").T for n in ("w1", "w2", "h1", "h2")], axis=0),
        "s_up": np.stack([a(f"L0_ffn_{n}_s").reshape(-1, 128).T for n in ("w1", "w2", "h1", "h2")], axis=1),
        "w_down_t": a("L0_ffn_w3_w").T,
        "s_down": a("L0_ffn_w3_s").reshape(1, -1),
    }
    nc = bacc.Bacc("TRN2", target_bir_lowering=False, num_devices=1)
    arrays, args = {}, []
    for name, value in in_map.items():
        value = np.ascontiguousarray(value)
        arrays[name + "_dram"] = value
        args.append(nc.dram_tensor(name + "_dram", value.shape, mb.dt.from_np(value.dtype),
                                   kind="ExternalInput").ap())
    x = in_map["x"]
    args.append(nc.dram_tensor("out_dram", x.shape, mb.dt.from_np(x.dtype), kind="ExternalOutput").ap())
    layer_kernel(nc, *args)
    r = run_bass_kernel_spmd(nc, [arrays], core_ids=[0])
    return r.results[0]["out_dram"]
```

```python
from contextlib import ExitStack

import concourse.bass as bass
from concourse import mybir

F32 = mybir.dt.float32
F32R = mybir.dt.float32r
BF16 = mybir.dt.bfloat16
I32 = mybir.dt.int32
U32 = mybir.dt.uint32
ALU = mybir.AluOpType
ACT = mybir.ActivationFunctionType
AX_X = mybir.AxisListType.X

P = 128
BANK = 512
EPS = 1e-5
NEG = -3.0e38


def layer_kernel(nc, x, w_basis_dup_t, w_v, w_o_t, b_v, b_o, w_mlp_t, s_mlp, s_down, out):
    T = x.shape[1]
    B = x.shape[0]
    C = x.shape[2]
    R = w_basis_dup_t.shape[1] // 2
    HID = w_mlp_t.shape[1]
    KC = HID // P
    NT = T // P
    HALVES = T // BANK
    G = B * T // BANK
    GT = BANK // P
    SCALE = float(R) ** -0.5
    assert C == P and 2 * R == P and HALVES == 2 and B % 2 == 0

    chunks = [(j, q, min(BANK, T - q)) for j in range(NT) for q in range(j * P, T, BANK)]
    NCH = len(chunks)
    chunks_to = [sum(c[0] <= j for c in chunks) for j in range(NT)]
    probs_at = [sum(T - i * P for i in range(j)) for j in range(NT)]
    probs_cols = sum(T - j * P for j in range(NT))
    max_chunks = [(t, k, min(BANK, (t + 1) * P - k)) for t in reversed(range(NT))
                  for k in range(0, (t + 1) * P, BANK)]
    NMX = len(max_chunks)
    W1, W2, WH1, WH2, W3 = 0, 1, 2, 2 + KC, 2 + 2 * KC
    WK = W3 + 1
    W_STEP = 3
    w_late = range(W_STEP * (B // 2 - 1), WK)
    assert w_mlp_t.shape[0] == WK * P and KC * C == HID

    with ExitStack() as ctx:
        def sb(name, shape, dt=F32, scope=ctx):
            return scope.enter_context(nc.sbuf_tensor(name, shape, dt))

        def sem(name):
            return ctx.enter_context(nc.semaphore(name))

        x_sb = sb("x_sb", [P, B * NT, C])
        w_hi = sb("w_hi", [P, WK, HID], F32R)
        w_lo = sb("w_lo", [P, WK, HID], F32R)
        scales = sb("scales", [P, 4, KC])
        s_down_col = sb("s_down_col", [P, 1])
        ident = sb("ident", [P, P])
        ident_bf = sb("ident_bf", [P, P], BF16)
        mask_q = sb("mask_q", [P, P], BF16)
        mask_k = sb("mask_k", [P, P], BF16)
        ones = sb("ones", [P, 2])
        lo_max = sb("lo_max", [P, 1])
        lo_flag = sb("lo_flag", [1, 1], I32)
        bn = sb("bn", [P, NT, 6])
        ln_mean = sb("ln_mean", [P, NT])
        ln_var = sb("ln_var", [P, NT])
        ln_rstd = sb("ln_rstd", [P, NT])
        ln_t = sb("ln_t", [P, NT])
        ln_bias = sb("ln_bias", [P, NT])
        post_bn = sb("post_bn", [P, NT, 6])
        post_mean = sb("post_mean", [P, NT])
        post_v = sb("post_v", [P, NT])
        post_r2 = sb("post_r2", [P, NT])
        post_rstd = sb("post_rstd", [P, NT])
        post_t = sb("post_t", [P, NT])
        minus_half = sb("minus_half", [P, NT])
        o_sb = [sb(f"o_sb{p}", [P, NT, C + 1]) for p in range(2)]
        o_ln = sb("o_ln", [P, NT, C])
        xn2 = sb("xn2", [P, GT, C])
        xt_hi = sb("xt_hi", [P, 1, BANK], F32R)
        xt_lo = sb("xt_lo", [P, 1, BANK], F32R)

        with ExitStack() as one:
            w_raw = sb("w_raw", [P, WK, HID], F32, one)
            w_basis = sb("w_basis", [P, P], F32, one)
            w_v_sb = sb("w_v_sb", [P, P], F32, one)
            w_o_sb = sb("w_o_sb", [P, P], F32, one)
            w_vo = sb("w_vo", [P, P], F32, one)
            b_v_col = sb("b_v_col", [P, 1], F32, one)
            b_v_bc = sb("b_v_bc", [P, P], F32, one)
            b_o_bc = sb("b_o_bc", [P, P], F32, one)
            b_vo_bc = sb("b_vo_bc", [P, P], F32, one)
            xn = sb("xn", [P, NT, C], F32, one)
            xt = sb("xt", [P, T], F32, one)
            lat_hh = [sb(f"lat_hh{p}", [P, T], F32R, one) for p in range(2)]
            lat_hl = [sb(f"lat_hl{p}", [P, T], F32R, one) for p in range(2)]
            lat_l1 = [sb(f"lat_l1{p}", [R + 1, T], F32R, one) for p in range(2)]
            lat_hm = [sb(f"lat_hm{p}", [R + 1, T], F32R, one) for p in range(2)]
            values = [sb(f"values{p}", [P, NT, C + 1], F32, one) for p in range(2)]
            probs = sb("probs", [P, probs_cols], F32, one)
            row_max = sb("row_max", [P, 2, NT], F32, one)
        with ExitStack() as two:
            gate = sb("gate", [P, 2, BANK], F32, two)
            h1_full = sb("h1_full", [P, KC, BANK], F32, two)
            h2_full = sb("h2_full", [P, 2, BANK], F32, two)
            h1_hi = sb("h1_hi", [P, KC, BANK], F32R, two)
            h1_lo = sb("h1_lo", [P, KC, BANK], F32R, two)
            h2_hi = sb("h2_hi", [P, KC, BANK], F32R, two)
            h2_lo = sb("h2_lo", [P, KC, BANK], F32R, two)
            h3_full = sb("h3_full", [P, 2, BANK], F32, two)
            h3_hi = sb("h3_hi", [P, KC, BANK], F32R, two)
            h3_lo = sb("h3_lo", [P, KC, BANK], F32R, two)
            yt = sb("yt", [P, BANK], F32, two)
            y_ln = sb("y_ln", [P, GT, C], F32, two)

        with ExitStack() as one:
            ps = lambda name, shape: one.enter_context(nc.psum_tensor(name, shape, F32))
            ps_prep = ps("ps_prep", [P, 2, BANK])
            ps_max = ps("ps_max", [P, 2, BANK])
            ps_s = ps("ps_s", [P, 2, BANK])
            ps_o = ps("ps_o", [P, 2, BANK])
        with ExitStack() as two:
            ps = lambda name, shape: two.enter_context(nc.psum_tensor(name, shape, F32))
            ps_t = ps("ps_t", [P, GT, P])
            ps_y = ps("ps_y", [P, GT, P])
            ps_g = ps("ps_g", [P, 2, BANK])
            ps_u = ps("ps_u", [P, 2, BANK])
            ps_h = ps("ps_h", [P, 2, BANK])

        consts_ready = sem("consts_ready")
        w_attn_loaded = sem("w_attn_loaded")
        w_mlp_loaded = sem("w_mlp_loaded")
        s_loaded = sem("s_loaded")
        x_loaded = sem("x_loaded")
        out_stored = sem("out_stored")
        setup_pe = sem("setup_pe")
        setup_dve = sem("setup_dve")
        pool_step = sem("pool_step")
        w_hi_ready = sem("w_hi_ready")
        w_lo_ready = sem("w_lo_ready")
        flag_step = sem("flag_step")
        ln1_step = sem("ln1_step")
        ln1_var = sem("ln1_var")
        ln1_rstd = sem("ln1_rstd")
        ln1_ready = sem("ln1_ready")
        xn_ready = sem("xn_ready")
        t_done = sem("t_done")
        xt_ready = sem("xt_ready")
        lat_done = sem("lat_done")
        hi_ready = sem("hi_ready")
        hm_ready = sem("hm_ready")
        lo_ready = sem("lo_ready")
        val_done = sem("val_done")
        val_ready = sem("val_ready")
        max_scores_done = sem("max_scores_done")
        max_ready = sem("max_ready")
        max_joined = sem("max_joined")
        max_row_done = sem("max_row_done")
        max_row_ready = sem("max_row_ready")
        scores_done = sem("scores_done")
        probs_ready = sem("probs_ready")
        o_done = sem("o_done")
        o_ready = sem("o_ready")
        post_step = sem("post_step")
        post_var = sem("post_var")
        post_ready = sem("post_ready")
        o_ln_ready = sem("o_ln_ready")
        x1_ready = sem("x1_ready")
        both_step = sem("both_step")
        both_var = sem("both_var")
        both_ready = sem("both_ready")
        xn2_ready = sem("xn2_ready")
        t2_done = sem("t2_done")
        xt2_hi_ready = sem("xt2_hi_ready")
        xt2_ready = sem("xt2_ready")
        g_done = sem("g_done")
        u_done = sem("u_done")
        gate_ready = sem("gate_ready")
        gated = sem("gated")
        h1_hi_ready = sem("h1_hi_ready")
        h1_ready = sem("h1_ready")
        h2_done = sem("h2_done")
        h2_act = sem("h2_act")
        h2_hi_ready = sem("h2_hi_ready")
        h2_ready = sem("h2_ready")
        h3_done = sem("h3_done")
        h3_act = sem("h3_act")
        h3_hi_ready = sem("h3_hi_ready")
        h3_ready = sem("h3_ready")
        y_done = sem("y_done")
        yt_ready = sem("yt_ready")
        y_back = sem("y_back")
        y_ln_ready = sem("y_ln_ready")
        out_ready = sem("out_ready")

        class Steps:

            def __init__(self, eng, semaphore, base):
                self.eng, self.sem, self.value = eng, semaphore, base

            def then(self, ins):
                ins.then_inc(self.sem, 1)
                self.value = self.value + 1
                self.eng.wait_ge(self.sem, self.value)

        def aggregate(v, steps, stats, mean, var, d, eps):
            n = C // 2
            v.tensor_tensor(mean, stats[:, :, 1], stats[:, :, 4], ALU.add)
            steps.then(v.tensor_tensor(d, stats[:, :, 1], stats[:, :, 4], ALU.subtract))
            v.tensor_scalar(mean, mean, 0.5, None, ALU.mult)
            v.scalar_tensor_tensor(out=var, in0=stats[:, :, 2], scalar=2 * n * eps,
                                   in1=stats[:, :, 5], op0=ALU.add, op1=ALU.add)
            steps.then(v.scalar_tensor_tensor(out=d, in0=d, scalar=0.25, in1=d, op0=ALU.mult, op1=ALU.mult))
            return v.scalar_tensor_tensor(out=var, in0=var, scalar=0.5 / n, in1=d,
                                          op0=ALU.mult, op1=ALU.add)

        AGGREGATE_STEPS = 2
        x_cols, y_cols = slice(0, GT), slice(GT, 2 * GT)
        LN1_STEPS = 2 + AGGREGATE_STEPS
        POST_STEPS = 1 + AGGREGATE_STEPS + 1
        BOTH_STEPS = 1 + AGGREGATE_STEPS

        block = ctx.enter_context(nc.Block())

        @block.sync
        def _(sp):
            xr = x.rearrange("b (t p) c -> b p t c", p=P)

            def load_x(b, b_dram):
                sp.dma_start(x_sb[:, bass.ts(b, NT), :], xr[b_dram]).then_inc(x_loaded, 16)

            load_x(0, 0)
            for dst, src in ((w_basis[:], w_basis_dup_t), (w_v_sb[:], w_v), (w_o_sb[:], w_o_t),
                             (b_v_col[:], b_v), (b_o_bc[:], b_o.to_broadcast([P, C]))):
                sp.dma_start(dst, src).then_inc(w_attn_loaded, 16)
            for b in range(1, B):
                sp.wait_ge(x_loaded, 16 * b)
                load_x(b, b)
                if b == 2:
                    sp.dma_start(w_raw[:], w_mlp_t.rearrange("(k p) n -> p k n", p=P)).then_inc(w_mlp_loaded, 16)
            sp.dma_start(scales[:], s_mlp).then_inc(s_loaded, 16)
            sp.dma_start(s_down_col[:], s_down).then_inc(s_loaded, 16)
            outr = out.rearrange("b (h t p) c -> (b h) p t c", p=P, t=GT)
            with sp.Fori(0, G) as g:
                sp.wait_ge(out_ready, g + 1)
                sp.dma_start(outr[bass.ds(g, 1)].rearrange("g p t c -> (g p) t c"),
                             x_sb[:, bass.ts(g, GT), :]).then_inc(out_stored, 16)
            sp.wait_ge(out_stored, 16 * G)

        @block.gpsimd
        def _(pool):
            st = Steps(pool, pool_step, 0)
            st.then(pool.memset(ident[:], 0.0))
            st.then(pool.affine_select(out=ident[:], in_=ident[:], compare_op=ALU.not_equal, fill=1.0,
                                       base=0, pattern=[[-1, P]], channel_multiplier=1))
            st.then(pool.tensor_copy(ident_bf[:], ident[:]))
            st.then(pool.memset(mask_q[:], 0.0))
            st.then(pool.affine_select(out=mask_q[:], in_=mask_q[:], compare_op=ALU.is_ge, fill=NEG,
                                       base=0, pattern=[[-1, P]], channel_multiplier=1))
            st.then(pool.memset(mask_k[:], 0.0))
            st.then(pool.affine_select(out=mask_k[:], in_=mask_k[:], compare_op=ALU.is_ge, fill=NEG,
                                       base=0, pattern=[[1, P]], channel_multiplier=-1))
            st.then(pool.memset(ones[:], 1.0))
            for p in range(2):
                st.then(pool.memset(values[p][:, :, C:C + 1], 1.0))
                st.then(pool.memset(lat_l1[p][R:R + 1, :].bitcast(F32), 1.0))
            pool.memset(minus_half[:], -0.5).then_inc(consts_ready, 1)

            def copy_hm(b, p):
                for h in range(HALVES):
                    s = slice(h * BANK, (h + 1) * BANK)
                    pool.wait_ge(hi_ready, HALVES * b + h + 1)
                    pool.tensor_tensor(lat_hm[p][0:R, s], lat_hh[p][0:R, s].bitcast(F32),
                                       ones[0:R, 0:1].to_broadcast([R, BANK]),
                                       ALU.mult).then_inc(hm_ready, 1)

            def rstd1(b):
                pool.wait_ge(ln1_var, b + 1)
                pool.tensor_tensor(ln_rstd[:], ln_var[:], minus_half[:], ALU.pow).then_inc(ln1_rstd, 1)

            def rstd_post(b):
                pool.wait_ge(post_var, b + 1)
                pool.tensor_tensor(post_rstd[:], post_v[:], minus_half[:], ALU.pow).then_inc(post_ready, 1)

            def add_x1(b):
                pool.wait_ge(o_ln_ready, b + 1)
                xs = x_sb[:, bass.ts(b, NT), :]
                pool.tensor_tensor(xs, xs, o_ln[:], ALU.add).then_inc(x1_ready, 1)

            def lo_weights(k):
                pool.wait_ge(w_hi_ready, k + 1)
                w = bass.ds(k, 1)
                pool.tensor_tensor(w_lo[:, w], w_raw[:, w], w_hi[:, w].bitcast(F32),
                                   ALU.subtract).then_inc(w_lo_ready, 1)

            pool.wait_ge(consts_ready, 1)
            rstd1(0)
            rstd1(1)
            copy_hm(0, 0)
            with pool.Fori(0, B // 2 - 1) as i:
                for p in range(2):
                    b = 2 * i + p
                    copy_hm(b + 1, 1 - p)
                    rstd1(b + 2)
                    for k in range(2 - p):
                        lo_weights(W_STEP * i + 2 * p + k)
                    rstd_post(b)
                    add_x1(b)
            copy_hm(B - 1, 1)
            for k in w_late:
                lo_weights(k)
            rstd_post(B - 2)
            add_x1(B - 2)

            def rstd_both(n, cols=slice(None)):
                pool.wait_ge(both_var, n + 1)
                pool.tensor_tensor(ln_rstd[:, cols], ln_var[:, cols], minus_half[:, cols],
                                   ALU.pow).then_inc(both_ready, 1)

            def add_y(g):
                pool.wait_ge(y_ln_ready, g + 1)
                xs = x_sb[:, bass.ts(g, GT), :]
                pool.tensor_tensor(xs, xs, y_ln[:], ALU.add).then_inc(out_ready, 1)

            rstd_both(0)
            rstd_post(B - 1)
            rstd_both(1, x_cols)
            add_x1(B - 1)
            rstd_both(2, x_cols)
            with pool.Fori(2, G - 2) as g:
                rstd_both(g + 1)
                add_y(g - 2)
            for g in range(G - 2, G + 2):
                rstd_both(g + 1, y_cols)
                add_y(g - 2)

        @block.scalar
        def _(act):
            def normalise(b):
                act.wait_ge(ln1_ready, b + 1)
                for t in range(NT):
                    ins = act.activation(xn[:, t, :], x_sb[:, bass.ds(b * NT + t, 1), :],
                                         ACT.Identity, bias=ln_bias[:, t:t + 1], scale=ln_rstd[:, t:t + 1])
                    if (t + 1) * P % BANK == 0:
                        ins.then_inc(xn_ready, 1)

            def copy_xt(b):
                for h in range(HALVES):
                    act.wait_ge(t_done, HALVES * b + h + 1)
                    act.copy(xt[:, h * BANK:(h + 1) * BANK], ps_prep[:, h, :]).then_inc(xt_ready, 1)

            def round_lat(b, p):
                for h in range(HALVES):
                    act.wait_ge(lat_done, HALVES * b + h + 1)
                    act.copy(lat_hh[p][:, h * BANK:(h + 1) * BANK], ps_prep[:, h, :]).then_inc(hi_ready, 1)

            def exp(b, j):
                for n, (jj, q, width) in enumerate(chunks):
                    if jj == j:
                        act.wait_ge(scores_done, NCH * b + n + 1)
                        at = probs_at[j] + q - j * P
                        act.activation(probs[:, at:at + width], ps_s[:, n % 2, 0:width], ACT.Exp,
                                       scale=SCALE).then_inc(probs_ready, 1)

            def copy_o(b, p, t):
                act.wait_ge(o_done, NT * b + t + 1)
                act.copy(o_sb[p][:, t, :], ps_o[:, t % 2, 0:C + 1]).then_inc(o_ready, 1)

            def copy_max_row(b, p):
                for h in range(HALVES):
                    act.wait_ge(max_row_done, HALVES * b + h + 1)
                    act.mul(lat_hm[p][R:R + 1, h * BANK:(h + 1) * BANK], ps_prep[R:R + 1, h, :],
                            -1.0).then_inc(max_row_ready, 1)

            def hi_weights(k):
                act.wait_ge(w_mlp_loaded, 16)
                w = bass.ds(k, 1)
                act.copy(w_hi[:, w], w_raw[:, w]).then_inc(w_hi_ready, 1)

            def step(b, p, prep, weights=()):
                if prep:
                    copy_xt(b + 1)
                exp(b, 0)
                if prep:
                    round_lat(b + 1, 1 - p)
                exp(b, 1)
                exp(b, 2)
                copy_o(b, p, 0)
                exp(b, 3)
                copy_o(b, p, 1)
                exp(b, 4)
                copy_o(b, p, 2)
                for k in weights:
                    hi_weights(k)
                copy_o(b, p, 3)
                exp(b, 5)
                if prep and not isinstance(b, int):
                    normalise(b + 2)
                copy_o(b, p, 4)
                exp(b, 6)
                copy_o(b, p, 5)
                exp(b, 7)
                copy_o(b, p, 6)
                if prep:
                    copy_max_row(b + 1, 1 - p)
                copy_o(b, p, 7)

            normalise(0)
            copy_xt(0)
            round_lat(0, 0)
            normalise(1)
            copy_max_row(0, 0)
            with act.Fori(0, B // 2 - 1) as i:
                step(2 * i, 0, True, [W_STEP * i, W_STEP * i + 1])
                step(2 * i + 1, 1, True, [W_STEP * i + 2])
            step(B - 2, 0, True, w_late)
            step(B - 1, 1, False)

            def round_xt(g):
                act.wait_ge(t2_done, g + 1)
                act.copy(xt_hi[:, 0, :], ps_t[:].rearrange("p t c -> p (t c)")).then_inc(xt2_hi_ready, 1)

            def silu(g, c):
                act.wait_ge(g_done, KC * g + c + 1)
                act.activation(gate[:, c % 2, :], ps_g[:, c % 2, :], ACT.Silu,
                               scale=scales[:, 0, c:c + 1]).then_inc(gate_ready, 1)

            def hi_h1(g, c):
                act.wait_ge(gated, KC * g + c + 1)
                act.copy(h1_hi[:, c, :], h1_full[:, c, :]).then_inc(h1_hi_ready, 1)

            def gelu2(g):
                for c in range(KC):
                    act.wait_ge(h2_done, KC * g + c + 1)
                    if c >= 2:
                        act.wait_ge(h2_ready, KC * g + c - 1)
                    act.activation(h2_full[:, c % 2, :], ps_h[:, c % 2, :], ACT.Gelu,
                                   scale=scales[:, 2, c:c + 1]).then_inc(h2_act, 1)
                    act.wait_ge(h2_act, KC * g + c + 1)
                    act.copy(h2_hi[:, c, :], h2_full[:, c % 2, :]).then_inc(h2_hi_ready, 1)

            def gelu3(g, c):
                act.wait_ge(h3_done, KC * g + c + 1)
                if c >= 2:
                    act.wait_ge(h3_ready, KC * g + c - 1)
                act.activation(h3_full[:, c % 2, :], ps_h[:, c % 2, :], ACT.Gelu,
                               scale=scales[:, 3, c:c + 1]).then_inc(h3_act, 1)

            def hi_h3(g, c):
                act.wait_ge(h3_act, KC * g + c + 1)
                act.copy(h3_hi[:, c, :], h3_full[:, c % 2, :]).then_inc(h3_hi_ready, 1)

            def scale_y(g):
                act.wait_ge(y_done, g + 1)
                act.activation(yt[:], ps_y[:].rearrange("p t n -> p (t n)"), ACT.Copy,
                               scale=s_down_col[:, 0:1]).then_inc(yt_ready, 1)

            def mlp_step(g, has_t=True, has_3=True, has_y=True):
                if has_y:
                    scale_y(g - 2)
                silu(g, 0)
                silu(g, 1)
                hi_h1(g, 0)
                silu(g, 2)
                hi_h1(g, 1)
                silu(g, 3)
                hi_h1(g, 2)
                if has_3:
                    gelu3(g - 1, 0)
                hi_h1(g, 3)
                if has_3:
                    hi_h3(g - 1, 0)
                if has_t:
                    round_xt(g + 1)
                if has_3:
                    for c in range(1, KC):
                        gelu3(g - 1, c)
                        hi_h3(g - 1, c)
                gelu2(g)

            assert KC == 4
            round_xt(0)
            act.wait_ge(s_loaded, 32)
            mlp_step(0, has_3=False, has_y=False)
            mlp_step(1, has_y=False)
            with act.Fori(2, G - 1) as g:
                mlp_step(g)
            mlp_step(G - 1, has_t=False)
            scale_y(G - 2)
            for c in range(KC):
                gelu3(G - 1, c)
                hi_h3(G - 1, c)
            scale_y(G - 1)

        @block.vector
        def _(v):
            def setup():
                v.wait_ge(w_attn_loaded, 80)
                v.tensor_copy(b_v_bc[:], b_v_col[:].to_broadcast([P, P])).then_inc(setup_dve, 1)
                v.wait_ge(setup_pe, 1)
                v.tensor_copy(w_vo[:], ps_prep[:, 0, 0:P]).then_inc(setup_dve, 1)
                v.wait_ge(setup_pe, 2)
                v.tensor_tensor(b_vo_bc[:], ps_prep[:, 1, 0:P], b_o_bc[:], ALU.add).then_inc(setup_dve, 1)

            half_tiles = [list(range(NT // 2)), list(range(NT // 2, NT))]

            def ln1_stats(b, half):
                if half == 0:
                    v.wait_ge(x_loaded, 16 * (b + 1))
                for t in half_tiles[half]:
                    ins = v.bn_stats(bn[:, t, :], x_sb[:, bass.ds(b * NT + t, 1), :])
                ins.then_inc(ln1_step, 1)

            def ln1_variance(b):
                v.wait_ge(ln1_step, LN1_STEPS * b + 2)
                aggregate(v, Steps(v, ln1_step, LN1_STEPS * b + 2), bn[:], ln_mean[:], ln_var[:],
                          ln_t[:], EPS).then_inc(ln1_var, 1)

            def ln1_scale(b):
                v.wait_ge(ln1_rstd, b + 1)
                v.scalar_tensor_tensor(out=ln_bias[:], in0=ln_mean[:], scalar=-1.0, in1=ln_rstd[:],
                                       op0=ALU.mult, op1=ALU.mult).then_inc(ln1_ready, 1)

            def lo_lat(b, p):
                for h in range(HALVES):
                    s = slice(h * BANK, (h + 1) * BANK)
                    v.wait_ge(hi_ready, HALVES * b + h + 1)
                    v.tensor_copy(lat_hl[p][0:R, s], lat_hh[p][0:R, s])
                    v.tensor_tensor(lat_hl[p][R:P, s], ps_prep[R:P, h, :],
                                    lat_hh[p][R:P, s].bitcast(F32), ALU.subtract)
                    v.tensor_tensor(lat_l1[p][0:R, s], ps_prep[0:R, h, :],
                                    lat_hh[p][0:R, s].bitcast(F32), ALU.subtract).then_inc(lo_ready, 1)

            def bias_values(b, p):
                for h in range(HALVES):
                    v.wait_ge(val_done, HALVES * b + h + 1)
                    n = BANK // P
                    v.tensor_tensor(values[p][:, h * n:(h + 1) * n, 0:C],
                                    ps_prep[:, h, :].rearrange("p (t c) -> p t c", c=C),
                                    b_vo_bc[:].unsqueeze(1).to_broadcast([P, n, C]),
                                    ALU.add).then_inc(val_ready, 1)

            def take_max(b, n):
                t, k, width = max_chunks[n]
                v.wait_ge(max_scores_done, NMX * b + n + 1)
                v.reduce_max(row_max[:, k // BANK, t:t + 1], ps_max[:, n % 2, 0:width],
                             AX_X).then_inc(max_ready, 1)

            def join_max(b):
                v.wait_ge(max_ready, NMX * (b + 1))
                two = slice(BANK // P, NT)
                v.tensor_tensor(row_max[:, 0, two], row_max[:, 0, two], row_max[:, 1, two],
                                ALU.max).then_inc(max_joined, 1)

            def post_stats(b, p, tiles):
                for t in tiles:
                    v.wait_ge(o_ready, NT * b + t + 1)
                    ins = v.bn_stats(post_bn[:, t, :], o_sb[p][:, t, 0:C])
                return ins

            def post_variance(b, p, ins):
                st = Steps(v, post_step, POST_STEPS * b)
                st.then(ins)
                r = o_sb[p][:, :, C]
                v.scalar_tensor_tensor(out=post_r2[:], in0=r, scalar=EPS, in1=r,
                                       op0=ALU.mult, op1=ALU.mult)
                st.then(aggregate(v, st, post_bn[:], post_mean[:], post_v[:], post_t[:], 0.0))
                v.tensor_tensor(post_v[:], post_v[:], post_r2[:], ALU.add).then_inc(post_var, 1)

            def post_normalise(b, p, last=False):
                v.wait_ge(post_ready, b + 1)
                if last:
                    v.wait_ge(x1_ready, b)
                for t in range(NT):
                    ins = v.tensor_scalar(o_ln[:, t, :], o_sb[p][:, t, 0:C], post_mean[:, t:t + 1],
                                          post_rstd[:, t:t + 1], ALU.subtract, ALU.mult)
                ins.then_inc(o_ln_ready, 1)

            def prep_step(b, p, norm):
                lo_lat(b + 1, 1 - p)
                take_max(b + 1, 0)
                take_max(b + 1, 1)
                if norm:
                    ln1_stats(b + 2, 0)
                bias_values(b + 1, 1 - p)
                take_max(b + 1, 2)
                if norm:
                    ln1_stats(b + 2, 1)
                take_max(b + 1, 3)
                if norm:
                    ln1_variance(b + 2)
                take_max(b + 1, 4)
                post_stats(b, p, range(0, 2))
                if norm:
                    ln1_scale(b + 2)
                post_stats(b, p, range(2, 4))
                for n in range(5, 8):
                    take_max(b + 1, n)
                post_stats(b, p, [4])
                take_max(b + 1, 8)
                post_stats(b, p, [5])
                for n in range(9, NMX):
                    take_max(b + 1, n)
                join_max(b + 1)
                post_variance(b, p, post_stats(b, p, [6, 7]))
                post_normalise(b, p)

            def x1_stats(g, first):
                for t in range(GT):
                    ins = v.bn_stats(bn[:, first + t, :], x_sb[:, bass.ds(g * GT + t, 1), :])
                return ins

            def both_variance(n, ins, cols=slice(None)):
                st = Steps(v, both_step, BOTH_STEPS * n)
                st.then(ins)
                aggregate(v, st, bn[:, cols], ln_mean[:, cols], ln_var[:, cols], ln_t[:, cols],
                          EPS).then_inc(both_var, 1)

            def normalise_x1(g, first=0):
                for t in range(GT):
                    a = first + t
                    ins = v.tensor_scalar(xn2[:, t, :], x_sb[:, bass.ds(g * GT + t, 1), :],
                                          ln_mean[:, a:a + 1], ln_rstd[:, a:a + 1],
                                          ALU.subtract, ALU.mult)
                ins.then_inc(xn2_ready, 1)

            def lo_xt(g):
                v.wait_ge(xt2_hi_ready, g + 1)
                v.tensor_tensor(xt_lo[:, 0, :], ps_t[:].rearrange("p t c -> p (t c)"),
                                xt_hi[:, 0, :].bitcast(F32), ALU.subtract).then_inc(xt2_ready, 1)

            def gate_h1(g, c):
                v.wait_ge(gate_ready, KC * g + c + 1)
                v.wait_ge(u_done, KC * g + c + 1)
                v.scalar_tensor_tensor(out=h1_full[:, c, :], in0=ps_u[:, c % 2, :],
                                       scalar=scales[:, 1, c:c + 1], in1=gate[:, c % 2, :],
                                       op0=ALU.mult, op1=ALU.mult).then_inc(gated, 1)

            def lo_h1(g, c):
                v.wait_ge(h1_hi_ready, KC * g + c + 1)
                v.tensor_tensor(h1_lo[:, c, :], h1_full[:, c, :], h1_hi[:, c, :].bitcast(F32),
                                ALU.subtract).then_inc(h1_ready, 1)

            def lo_h2(g, c):
                v.wait_ge(h2_hi_ready, KC * g + c + 1)
                v.tensor_tensor(h2_lo[:, c, :], h2_full[:, c % 2, :], h2_hi[:, c, :].bitcast(F32),
                                ALU.subtract).then_inc(h2_ready, 1)

            def lo_h3(g, c):
                v.wait_ge(h3_hi_ready, KC * g + c + 1)
                v.tensor_tensor(h3_lo[:, c, :], h3_full[:, c % 2, :], h3_hi[:, c, :].bitcast(F32),
                                ALU.subtract).then_inc(h3_ready, 1)

            def y_stats(g):
                v.wait_ge(y_back, g + 1)
                for t in range(GT):
                    ins = v.bn_stats(bn[:, GT + t, :], ps_y[:, t, :])
                return ins

            def normalise_y(g, first=False):
                if not first:
                    v.wait_ge(out_ready, g)
                for t in range(GT):
                    a = GT + t
                    ins = v.tensor_scalar(y_ln[:, t, :], ps_y[:, t, :], ln_mean[:, a:a + 1],
                                          ln_rstd[:, a:a + 1], ALU.subtract, ALU.mult)
                ins.then_inc(y_ln_ready, 1)

            def mlp_step(g, has_x=True, has_3=True, has_y=True, last_post=False, wait_x1=False):
                gate_h1(g, 0)
                gate_h1(g, 1)
                lo_h1(g, 0)
                if has_y:
                    ins = y_stats(g - 2)
                gate_h1(g, 2)
                lo_h1(g, 1)
                gate_h1(g, 3)
                lo_h1(g, 2)
                if wait_x1:
                    v.wait_ge(x1_ready, B)
                if has_x:
                    ins = x1_stats(g + 2, 0)
                cols = slice(None) if has_x and has_y else x_cols if has_x else y_cols
                if last_post:
                    post_variance(B - 1, 1, post_stats(B - 1, 1, range(NT)))
                both_variance(g + 1, ins, cols)
                lo_h1(g, 3)
                if has_3:
                    lo_h3(g - 1, 0)
                if not (isinstance(g, int) and g == G - 1):
                    lo_xt(g + 1)
                if last_post:
                    post_normalise(B - 1, 1, True)
                if has_3:
                    lo_h3(g - 1, 1)
                v.wait_ge(both_ready, g + 2)
                if has_y:
                    normalise_y(g - 2, isinstance(g, int) and g == 2)
                if has_3:
                    lo_h3(g - 1, 2)
                if has_x:
                    normalise_x1(g + 2)
                if has_3:
                    lo_h3(g - 1, 3)
                for c in range(KC):
                    lo_h2(g, c)

            for b in range(2):
                if b:
                    v.wait_ge(xn_ready, HALVES * b)
                ln1_stats(b, 0)
                ln1_stats(b, 1)
                ln1_variance(b)
                if b == 0:
                    setup()
                ln1_scale(b)
            lo_lat(0, 0)
            take_max(0, 0)
            take_max(0, 1)
            bias_values(0, 0)
            for n in range(2, NMX):
                take_max(0, n)
            join_max(0)
            with v.Fori(0, B // 2 - 1) as i:
                for p in range(2):
                    prep_step(2 * i + p, p, True)
            prep_step(B - 2, 0, False)

            both_variance(0, (x1_stats(0, 0), x1_stats(1, GT))[1])
            v.wait_ge(w_lo_ready, WK)
            v.tensor_reduce(lo_max[:], w_lo[:].rearrange("p k n -> p (k n)").bitcast(U32), AX_X,
                            ALU.max).then_inc(flag_step, 1)
            v.wait_ge(both_ready, 1)
            normalise_x1(0, 0)
            v.wait_ge(flag_step, 2)
            v.tensor_scalar(lo_flag[:], ps_prep[0:1, 1, 0:1], 0.0, None, ALU.is_gt).then_inc(flag_step, 1)
            lo_xt(0)
            normalise_x1(1, GT)

            v.wait_ge(s_loaded, 32)
            mlp_step(0, has_3=False, has_y=False, last_post=True)
            mlp_step(1, has_y=False, wait_x1=True)
            mlp_step(2)
            with v.Fori(3, G - 2) as g:
                mlp_step(g)
            mlp_step(G - 2, has_x=False)
            mlp_step(G - 1, has_x=False)
            lo_h3(G - 1, 0)
            both_variance(G + 1, y_stats(G - 2), y_cols)
            lo_h3(G - 1, 1)
            v.wait_ge(both_ready, G + 2)
            normalise_y(G - 2)
            lo_h3(G - 1, 2)
            lo_h3(G - 1, 3)
            both_variance(G + 2, y_stats(G - 1), y_cols)
            v.wait_ge(both_ready, G + 3)
            normalise_y(G - 1)

        @block.tensor
        def _(pe):
            pe.wait_ge(consts_ready, 1)
            pe.wait_ge(w_attn_loaded, 80)
            pe.matmul(ps_prep[:, 0, 0:P], w_v_sb[:], w_o_sb[:], start=True, stop=True).then_inc(setup_pe, 1)
            pe.wait_ge(setup_dve, 1)
            pe.matmul(ps_prep[:, 1, 0:P], b_v_bc[:], w_o_sb[:], start=True, stop=True).then_inc(setup_pe, 1)
            pe.wait_ge(setup_dve, 3)

            def transpose_x(b, first=False):
                if not first:
                    pe.wait_ge(max_row_ready, HALVES * b)
                for t in range(NT):
                    h, c = divmod(t * P, BANK)
                    if c == 0:
                        pe.wait_ge(xn_ready, HALVES * b + h + 1)
                    ins = pe.transpose(ps_prep[:, h, c:c + P], xn[:, t, :], ident[:])
                    if c + P == BANK:
                        ins.then_inc(t_done, 1)

            def latents(b):
                for h in range(HALVES):
                    pe.wait_ge(xt_ready, HALVES * b + h + 1)
                    pe.matmul(ps_prep[:, h, :], w_basis[:], xt[:, h * BANK:(h + 1) * BANK],
                              start=True, stop=True).then_inc(lat_done, 1)

            def make_values(b):
                pe.wait_ge(lo_ready, HALVES * (b + 1))
                for t in range(NT):
                    h, c = divmod(t * P, BANK)
                    ins = pe.matmul(ps_prep[:, h, c:c + P], xt[:, t * P:(t + 1) * P], w_vo[:],
                                    start=True, stop=True)
                    if c + P == BANK:
                        ins.then_inc(val_done, 1)

            def max_scores(b, p, n):
                t, k, width = max_chunks[n]
                if n == 0:
                    pe.wait_ge(lo_ready, HALVES * (b + 1))
                if n >= 2:
                    pe.wait_ge(max_ready, NMX * b + n - 1)
                end = (t + 1) * P
                own = k + width == end
                ins = pe.matmul(ps_max[:, n % 2, 0:width], lat_hh[p][:, t * P:end],
                                lat_hl[p][:, k:k + width], start=True, stop=not own)
                if own:
                    ins = pe.matmul(ps_max[:, n % 2, width - P:width], ident_bf[:], mask_q[:],
                                    start=False, stop=True)
                ins.then_inc(max_scores_done, 1)

            def lay_max(b):
                pe.wait_ge(max_joined, b + 1)
                pe.wait_ge(val_ready, HALVES * (b + 1))
                for t in range(NT):
                    h, c = divmod(t * P, BANK)
                    ins = pe.matmul(ps_prep[R:R + 1, h, c:c + P], row_max[:, 0, t:t + 1], ident[:],
                                    start=True, stop=True)
                    if c + P == BANK:
                        ins.then_inc(max_row_done, 1)

            def scores(b, p, j):
                if j == 0:
                    pe.wait_ge(max_row_ready, HALVES * (b + 1))
                    pe.wait_ge(hm_ready, HALVES * (b + 1))
                for n, (jj, q, width) in enumerate(chunks):
                    if jj != j:
                        continue
                    if n >= 2:
                        pe.wait_ge(probs_ready, NCH * b + n - 1)
                    own = q == j * P
                    k = slice(j * P, (j + 1) * P)
                    pe.matmul(ps_s[:, n % 2, 0:width], lat_hh[p][:, k], lat_hl[p][:, q:q + width],
                              start=True, stop=False)
                    ins = pe.matmul(ps_s[:, n % 2, 0:width], lat_l1[p][:, k], lat_hm[p][:, q:q + width],
                                    start=False, stop=not own)
                    if own:
                        ins = pe.matmul(ps_s[:, n % 2, 0:P], ident_bf[:], mask_k[:], start=False, stop=True)
                    ins.then_inc(scores_done, 1)

            def attend(b, p, t):
                pe.wait_ge(probs_ready, NCH * b + chunks_to[t])
                if t >= 2:
                    pe.wait_ge(o_ready, NT * b + t - 1)
                for j in range(t + 1):
                    at = probs_at[j] + (t - j) * P
                    ins = pe.matmul(ps_o[:, t % 2, 0:C + 1], probs[:, at:at + P], values[p][:, j, :],
                                    start=(j == 0), stop=(j == t))
                ins.then_inc(o_done, 1)

            def prep_step(b, p):
                def maxima(*ns):
                    for n in ns:
                        max_scores(b + 1, 1 - p, n)

                transpose_x(b + 1)
                scores(b, p, 0)
                latents(b + 1)
                scores(b, p, 1)
                attend(b, p, 0)
                scores(b, p, 2)
                attend(b, p, 1)
                scores(b, p, 3)
                attend(b, p, 2)
                scores(b, p, 4)
                maxima(0, 1)
                make_values(b + 1)
                maxima(2)
                attend(b, p, 3)
                maxima(3)
                scores(b, p, 5)
                maxima(4)
                attend(b, p, 4)
                maxima(5, 6)
                scores(b, p, 6)
                maxima(7)
                attend(b, p, 5)
                maxima(8, 9)
                scores(b, p, 7)
                maxima(10, 11)
                attend(b, p, 6)
                lay_max(b + 1)
                attend(b, p, 7)

            transpose_x(0, True)
            latents(0)
            max_scores(0, 0, 0)
            max_scores(0, 0, 1)
            make_values(0)
            for n in range(2, NMX):
                max_scores(0, 0, n)
            lay_max(0)
            with pe.Fori(0, B // 2 - 1) as i:
                for p in range(2):
                    prep_step(2 * i + p, p)
            prep_step(B - 2, 0)

            def transpose_x1(g):
                pe.wait_ge(xn2_ready, g + 1)
                for t in range(GT):
                    ins = pe.transpose(ps_t[:, t, :], xn2[:, t, :], ident[:])
                ins.then_inc(t2_done, 1)

            last = B - 1
            scores(last, 1, 0)
            scores(last, 1, 1)
            for t in range(NT):
                if t == NT - 2:
                    transpose_x1(0)
                if t == NT - 1:
                    pe.wait_ge(flag_step, 1)
                    pe.matmul(ps_prep[0:1, 1, 0:1], lo_max[:], ones[:, 0:1], start=True,
                              stop=True).then_inc(flag_step, 1)
                attend(last, 1, t)
                if t + 2 < NT:
                    scores(last, 1, t + 2)
            pe.wait_ge(flag_step, 3)
            any_lo = pe.value_load(lo_flag[0:1, 0:1], min_val=0, max_val=1)

            def product(bank, weights, hi, lo, general):
                for k, (chunk, cols) in enumerate(weights):
                    passes = [(w_hi, hi), (w_hi, lo)] + ([(w_lo, hi)] if general else [])
                    for n, (w, h) in enumerate(passes):
                        ins = pe.matmul(bank, w[:, chunk, cols], h[:, k, :], start=(k == 0 and n == 0),
                                        stop=(k == len(weights) - 1 and n == len(passes) - 1))
                return ins

            def columns(c):
                return slice(c * P, (c + 1) * P)

            def up(g, c, general):
                if c == 0:
                    pe.wait_ge(xt2_ready, g + 1)
                if c >= 2:
                    pe.wait_ge(gated, KC * g + c - 1)
                product(ps_g[:, c % 2, :], [(W1, columns(c))], xt_hi, xt_lo, general).then_inc(g_done, 1)
                product(ps_u[:, c % 2, :], [(W2, columns(c))], xt_hi, xt_lo, general).then_inc(u_done, 1)

            def hidden2(g, general, first=False):
                pe.wait_ge(h1_ready, KC * (g + 1))
                if first:
                    pe.wait_ge(o_ready, NT * B)
                for c in range(KC):
                    if c >= 2:
                        pe.wait_ge(h2_act, KC * g + c - 1)
                    elif not first:
                        pe.wait_ge(h3_act, KC * g + c - 1)
                    product(ps_h[:, c % 2, :], [(WH1 + k, columns(c)) for k in range(KC)], h1_hi, h1_lo,
                            general).then_inc(h2_done, 1)

            def hidden3(g, c, general):
                if c == 0:
                    pe.wait_ge(h2_ready, KC * (g + 1))
                if c >= 2:
                    pe.wait_ge(h3_act, KC * g + c - 1)
                product(ps_h[:, c % 2, :], [(WH2 + k, columns(c)) for k in range(KC)], h2_hi, h2_lo,
                        general).then_inc(h3_done, 1)

            def down(g, general, first=False):
                pe.wait_ge(h3_ready, KC * (g + 1))
                if not first:
                    pe.wait_ge(y_ln_ready, g)
                product(ps_y[:].rearrange("p t n -> p (t n)"), [(W3, columns(k)) for k in range(KC)],
                        h3_hi, h3_lo, general).then_inc(y_done, 1)

            def transpose_y(g):
                pe.wait_ge(yt_ready, g + 1)
                for t in range(GT):
                    ins = pe.transpose(ps_y[:, t, :], yt[:, t * P:(t + 1) * P], ident[:])
                ins.then_inc(y_back, 1)

            def mlp_step(g, general, has_t=True, has_3=True, has_y=True, first=False):
                up(g, 0, general)
                up(g, 1, general)
                if has_y:
                    transpose_y(g - 2)
                if has_t:
                    transpose_x1(g + 1)
                up(g, 2, general)
                up(g, 3, general)
                if has_3:
                    for c in range(KC):
                        hidden3(g - 1, c, general)
                hidden2(g, general, first)
                if has_3:
                    down(g - 1, general, not has_y)

            def mlp(general):
                mlp_step(0, general, has_3=False, has_y=False, first=True)
                mlp_step(1, general, has_y=False)
                with pe.Fori(2, G - 1) as g:
                    mlp_step(g, general)
                mlp_step(G - 1, general, has_t=False)
                for c in range(KC):
                    hidden3(G - 1, c, general)
                    if c == 1:
                        transpose_y(G - 2)
                down(G - 1, general)
                transpose_y(G - 1)

            with pe.If(any_lo):
                mlp(True)
            with pe.Else():
                mlp(False)


def kernel(**inputs):
    import numpy as np
    import concourse.bacc as bacc
    from concourse import mybir as mb
    from concourse.bass_utils import run_bass_kernel_spmd

    def a(name):
        return np.asarray(inputs[name])

    wb = a("L0_attn_W_basis").T
    names = ("w1", "w2", "h1", "h2")
    w3 = a("L0_ffn_w3_w").T.reshape(-1, 128, 128).transpose(1, 0, 2).reshape(128, -1)
    in_map = {
        "x": a("L0_attn_hidden_states"),
        "w_basis_dup_t": np.concatenate([wb, wb], axis=1),
        "w_v": a("L0_attn_W_v"),
        "w_o_t": a("L0_attn_W_o").T,
        "b_v": a("L0_attn_b_v").reshape(-1, 1),
        "b_o": a("L0_attn_b_o").reshape(1, -1),
        "w_mlp_t": np.concatenate([a(f"L0_ffn_{n}_w").T for n in names] + [w3], axis=0),
        "s_mlp": np.stack([a(f"L0_ffn_{n}_s").reshape(-1, 128).T for n in names], axis=1),
        "s_down": a("L0_ffn_w3_s").reshape(-1, 1),
    }
    nc = bacc.Bacc("TRN2", target_bir_lowering=False, num_devices=1)
    arrays, args = {}, []
    for name, value in in_map.items():
        value = np.ascontiguousarray(value)
        arrays[name + "_dram"] = value
        args.append(nc.dram_tensor(name + "_dram", value.shape, mb.dt.from_np(value.dtype),
                                   kind="ExternalInput").ap())
    x = in_map["x"]
    args.append(nc.dram_tensor("out_dram", x.shape, mb.dt.from_np(x.dtype), kind="ExternalOutput").ap())
    layer_kernel(nc, *args)
    r = run_bass_kernel_spmd(nc, [arrays], core_ids=[0])
    return r.results[0]["out_dram"]
```

```python
from contextlib import ExitStack

import concourse.bass as bass
from concourse import mybir

F32 = mybir.dt.float32
F32R = mybir.dt.float32r
BF16 = mybir.dt.bfloat16
I32 = mybir.dt.int32
U32 = mybir.dt.uint32
ALU = mybir.AluOpType
ACT = mybir.ActivationFunctionType
AX_X = mybir.AxisListType.X

P = 128
BANK = 512
EPS = 1e-5
NEG = -3.0e38


def layer_kernel(nc, x, w_basis_dup_t, w_v, w_o_t, b_v, b_o, w_mlp_t, s_mlp, s_down, out):
    T = x.shape[1]
    B = x.shape[0]
    C = x.shape[2]
    R = w_basis_dup_t.shape[1] // 2
    HID = w_mlp_t.shape[1]
    KC = HID // P
    NT = T // P
    HALVES = T // BANK
    G = B * T // BANK
    GT = BANK // P
    SCALE = float(R) ** -0.5
    assert C == P and 2 * R == P and HALVES == 2 and B % 2 == 0

    half_tiles = [range(NT // 2), range(NT // 2, NT)]
    chunks = [(j, q, min(BANK, T - q)) for j in range(NT) for q in range(j * P, T, BANK)]
    NCH = len(chunks)
    chunks_to = [sum(c[0] <= j for c in chunks) for j in range(NT)]
    probs_at = [sum(T - i * P for i in range(j)) for j in range(NT)]
    probs_cols = sum(T - j * P for j in range(NT))
    max_chunks = [(t, k, min(BANK, (t + 1) * P - k)) for t in reversed(range(NT))
                  for k in range(0, (t + 1) * P, BANK)]
    NMX = len(max_chunks)
    W1, W2, WH1, WH2, W3 = 0, 1, 2, 2 + KC, 2 + 2 * KC
    WK = W3 + 1
    W_STEP = 3
    w_late = range(W_STEP * (B // 2 - 1), WK)
    assert w_mlp_t.shape[0] == WK * P and KC * C == HID

    with ExitStack() as ctx:
        def sb(name, shape, dt=F32, scope=ctx):
            return scope.enter_context(nc.sbuf_tensor(name, shape, dt))

        def sem(name):
            return ctx.enter_context(nc.semaphore(name))

        x_sb = sb("x_sb", [P, B * NT, C])
        w_hi = sb("w_hi", [P, WK, HID], F32R)
        w_lo = sb("w_lo", [P, WK, HID], F32R)
        scales = sb("scales", [P, 4, KC])
        s_down_col = sb("s_down_col", [P, 1])
        ident = sb("ident", [P, P])
        ident_bf = sb("ident_bf", [P, P], BF16)
        mask_q = sb("mask_q", [P, P], BF16)
        mask_k = sb("mask_k", [P, P], BF16)
        ones = sb("ones", [P, 2])
        lo_max = sb("lo_max", [P, 1])
        lo_flag = sb("lo_flag", [1, 1], I32)
        bn = sb("bn", [P, NT, 6])
        ln_mean = sb("ln_mean", [P, NT])
        ln_var = sb("ln_var", [P, NT])
        ln_rstd = sb("ln_rstd", [P, NT])
        ln_t = sb("ln_t", [P, NT])
        ln_bias = sb("ln_bias", [P, NT])
        post_bn = sb("post_bn", [P, NT, 6])
        post_mean = sb("post_mean", [P, NT])
        post_v = sb("post_v", [P, NT])
        post_r2 = sb("post_r2", [P, NT])
        post_rstd = sb("post_rstd", [P, NT])
        post_t = sb("post_t", [P, NT])
        minus_half = sb("minus_half", [P, NT])
        o_sb = [sb(f"o_sb{p}", [P, NT, C + 1]) for p in range(2)]
        o_ln = sb("o_ln", [P, NT, C])
        xn2 = sb("xn2", [P, GT, C])
        xt_hi = sb("xt_hi", [P, 1, BANK], F32R)
        xt_lo = sb("xt_lo", [P, 1, BANK], F32R)

        with ExitStack() as one:
            w_raw = sb("w_raw", [P, WK, HID], F32, one)
            w_basis = sb("w_basis", [P, P], F32, one)
            w_v_sb = sb("w_v_sb", [P, P], F32, one)
            w_o_sb = sb("w_o_sb", [P, P], F32, one)
            w_vo = sb("w_vo", [P, P], F32, one)
            b_v_col = sb("b_v_col", [P, 1], F32, one)
            b_v_bc = sb("b_v_bc", [P, P], F32, one)
            b_o_bc = sb("b_o_bc", [P, P], F32, one)
            b_vo_bc = sb("b_vo_bc", [P, P], F32, one)
            xn = sb("xn", [P, NT, C], F32, one)
            xt = sb("xt", [P, T], F32, one)
            lat_hh = [sb(f"lat_hh{p}", [P, T], F32R, one) for p in range(2)]
            lat_hl = [sb(f"lat_hl{p}", [P, T], F32R, one) for p in range(2)]
            lat_l1 = [sb(f"lat_l1{p}", [R + 1, T], F32R, one) for p in range(2)]
            lat_hm = [sb(f"lat_hm{p}", [R + 1, T], F32R, one) for p in range(2)]
            values = [sb(f"values{p}", [P, NT, C + 1], F32, one) for p in range(2)]
            probs = sb("probs", [P, probs_cols], F32, one)
            row_max = sb("row_max", [P, 2, NT], F32, one)
        with ExitStack() as two:
            gate = sb("gate", [P, 2, BANK], F32, two)
            h1_full = sb("h1_full", [P, KC, BANK], F32, two)
            h2_full = sb("h2_full", [P, 2, BANK], F32, two)
            h1_hi = sb("h1_hi", [P, KC, BANK], F32R, two)
            h1_lo = sb("h1_lo", [P, KC, BANK], F32R, two)
            h2_hi = sb("h2_hi", [P, KC, BANK], F32R, two)
            h2_lo = sb("h2_lo", [P, KC, BANK], F32R, two)
            h3_full = sb("h3_full", [P, 2, BANK], F32, two)
            h3_hi = sb("h3_hi", [P, KC, BANK], F32R, two)
            h3_lo = sb("h3_lo", [P, KC, BANK], F32R, two)
            yt = sb("yt", [P, BANK], F32, two)
            y_ln = sb("y_ln", [P, GT, C], F32, two)

        with ExitStack() as one:
            ps = lambda name, shape: one.enter_context(nc.psum_tensor(name, shape, F32))
            ps_prep = ps("ps_prep", [P, 2, BANK])
            ps_max = ps("ps_max", [P, 2, BANK])
            ps_s = ps("ps_s", [P, 2, BANK])
            ps_o = ps("ps_o", [P, 2, BANK])
        with ExitStack() as two:
            ps = lambda name, shape: two.enter_context(nc.psum_tensor(name, shape, F32))
            ps_t = ps("ps_t", [P, GT, P])
            ps_y = ps("ps_y", [P, GT, P])
            ps_g = ps("ps_g", [P, 2, BANK])
            ps_u = ps("ps_u", [P, 2, BANK])
            ps_h = ps("ps_h", [P, 2, BANK])

        consts_ready = sem("consts_ready")
        w_attn_loaded = sem("w_attn_loaded")
        w_mlp_loaded = sem("w_mlp_loaded")
        s_loaded = sem("s_loaded")
        x0_loaded = [sem(f"x0_loaded{h}") for h in range(HALVES)]
        x_loaded = sem("x_loaded")
        out_stored = sem("out_stored")
        setup_pe = sem("setup_pe")
        setup_dve = sem("setup_dve")
        pool_step = sem("pool_step")
        w_hi_ready = sem("w_hi_ready")
        w_lo_ready = sem("w_lo_ready")
        flag_step = sem("flag_step")
        ln1_step = sem("ln1_step")
        ln1_var = sem("ln1_var")
        ln1_rstd = sem("ln1_rstd")
        ln1_ready = sem("ln1_ready")
        xn_ready = sem("xn_ready")
        xn_dve_ready = sem("xn_dve_ready")
        t_done = sem("t_done")
        xt_ready = sem("xt_ready")
        lat_done = sem("lat_done")
        hi_ready = sem("hi_ready")
        hm_ready = sem("hm_ready")
        lo_ready = sem("lo_ready")
        val_done = sem("val_done")
        val_ready = sem("val_ready")
        max_scores_done = sem("max_scores_done")
        max_ready = sem("max_ready")
        max_joined = sem("max_joined")
        max_row_done = sem("max_row_done")
        max_row_ready = sem("max_row_ready")
        scores_done = sem("scores_done")
        probs_ready = sem("probs_ready")
        o_done = sem("o_done")
        o_ready = sem("o_ready")
        post_step = sem("post_step")
        post_var = sem("post_var")
        post_ready = sem("post_ready")
        o_ln_ready = sem("o_ln_ready")
        x1_ready = sem("x1_ready")
        both_step = sem("both_step")
        both_var = sem("both_var")
        both_ready = sem("both_ready")
        xn2_ready = sem("xn2_ready")
        t2_done = sem("t2_done")
        xt2_hi_ready = sem("xt2_hi_ready")
        xt2_ready = sem("xt2_ready")
        g_done = sem("g_done")
        u_done = sem("u_done")
        gate_ready = sem("gate_ready")
        gated = sem("gated")
        h1_hi_ready = sem("h1_hi_ready")
        h1_ready = sem("h1_ready")
        h2_done = sem("h2_done")
        h2_act = sem("h2_act")
        h2_hi_ready = sem("h2_hi_ready")
        h2_ready = sem("h2_ready")
        h3_done = sem("h3_done")
        h3_act = sem("h3_act")
        h3_hi_ready = sem("h3_hi_ready")
        h3_ready = sem("h3_ready")
        y_done = sem("y_done")
        yt_ready = sem("yt_ready")
        y_back = sem("y_back")
        y_ln_ready = sem("y_ln_ready")
        out_ready = sem("out_ready")
        last_out_ready = sem("last_out_ready")

        class Steps:

            def __init__(self, eng, semaphore, base):
                self.eng, self.sem, self.value = eng, semaphore, base

            def then(self, ins):
                ins.then_inc(self.sem, 1)
                self.value = self.value + 1
                self.eng.wait_ge(self.sem, self.value)

        def aggregate(v, steps, stats, mean, var, d, eps):
            n = C // 2
            v.tensor_tensor(mean, stats[:, :, 1], stats[:, :, 4], ALU.add)
            steps.then(v.tensor_tensor(d, stats[:, :, 1], stats[:, :, 4], ALU.subtract))
            v.tensor_scalar(mean, mean, 0.5, None, ALU.mult)
            v.scalar_tensor_tensor(out=var, in0=stats[:, :, 2], scalar=2 * n * eps,
                                   in1=stats[:, :, 5], op0=ALU.add, op1=ALU.add)
            steps.then(v.scalar_tensor_tensor(out=d, in0=d, scalar=0.25, in1=d, op0=ALU.mult, op1=ALU.mult))
            return v.scalar_tensor_tensor(out=var, in0=var, scalar=0.5 / n, in1=d,
                                          op0=ALU.mult, op1=ALU.add)

        AGGREGATE_STEPS = 2
        x_cols, y_cols = slice(0, GT), slice(GT, 2 * GT)
        LN1_STEPS = 2 + AGGREGATE_STEPS
        POST_STEPS = 1 + AGGREGATE_STEPS + 1
        BOTH_STEPS = 1 + AGGREGATE_STEPS

        block = ctx.enter_context(nc.Block())

        @block.sync
        def _(sp):
            xr = x.rearrange("b (t p) c -> b p t c", p=P)

            for h in range(HALVES):
                s = half_tiles[h]
                sp.dma_start(x_sb[:, s.start:s.stop, :], xr[0, :, s.start:s.stop]).then_inc(x0_loaded[h], 16)
            for dst, src in ((w_basis[:], w_basis_dup_t), (w_v_sb[:], w_v), (w_o_sb[:], w_o_t),
                             (b_v_col[:], b_v), (b_o_bc[:], b_o.to_broadcast([P, C]))):
                sp.dma_start(dst, src).then_inc(w_attn_loaded, 16)
            for b in range(1, B):
                if b > 1:
                    sp.wait_ge(x_loaded, 16 * (b - 1))
                sp.dma_start(x_sb[:, bass.ts(b, NT), :], xr[b]).then_inc(x_loaded, 16)
                if b == 2:
                    sp.dma_start(w_raw[:], w_mlp_t.rearrange("(k p) n -> p k n", p=P)).then_inc(w_mlp_loaded, 16)
            sp.dma_start(scales[:], s_mlp).then_inc(s_loaded, 16)
            sp.dma_start(s_down_col[:], s_down).then_inc(s_loaded, 16)
            outr = out.rearrange("b (h t p) c -> (b h) p t c", p=P, t=GT)

            def store(g):
                sp.dma_start(outr[bass.ds(g, 1)].rearrange("g p t c -> (g p) t c"),
                             x_sb[:, bass.ts(g, GT), :]).then_inc(out_stored, 16)

            with sp.Fori(0, G - 1) as g:
                sp.wait_ge(out_ready, g + 1)
                store(g)
            sp.wait_ge(last_out_ready, 1)
            store(G - 1)
            sp.wait_ge(out_stored, 16 * G)

        @block.gpsimd
        def _(pool):
            st = Steps(pool, pool_step, 0)
            st.then(pool.memset(ident[:], 0.0))
            st.then(pool.affine_select(out=ident[:], in_=ident[:], compare_op=ALU.not_equal, fill=1.0,
                                       base=0, pattern=[[-1, P]], channel_multiplier=1))
            st.then(pool.tensor_copy(ident_bf[:], ident[:]))
            st.then(pool.memset(mask_q[:], 0.0))
            st.then(pool.affine_select(out=mask_q[:], in_=mask_q[:], compare_op=ALU.is_ge, fill=NEG,
                                       base=0, pattern=[[-1, P]], channel_multiplier=1))
            st.then(pool.memset(mask_k[:], 0.0))
            st.then(pool.affine_select(out=mask_k[:], in_=mask_k[:], compare_op=ALU.is_ge, fill=NEG,
                                       base=0, pattern=[[1, P]], channel_multiplier=-1))
            st.then(pool.memset(ones[:], 1.0))
            for p in range(2):
                st.then(pool.memset(values[p][:, :, C:C + 1], 1.0))
                st.then(pool.memset(lat_l1[p][R:R + 1, :].bitcast(F32), 1.0))
            pool.memset(minus_half[:], -0.5).then_inc(consts_ready, 1)

            def copy_hm(b, p):
                for h in range(HALVES):
                    s = slice(h * BANK, (h + 1) * BANK)
                    pool.wait_ge(hi_ready, HALVES * b + h + 1)
                    pool.tensor_tensor(lat_hm[p][0:R, s], lat_hh[p][0:R, s].bitcast(F32),
                                       ones[0:R, 0:1].to_broadcast([R, BANK]),
                                       ALU.mult).then_inc(hm_ready, 1)

            def rstd1(b):
                pool.wait_ge(ln1_var, b + 1)
                pool.tensor_tensor(ln_rstd[:], ln_var[:], minus_half[:], ALU.pow).then_inc(ln1_rstd, 1)

            def rstd_post(b):
                pool.wait_ge(post_var, b + 1)
                pool.tensor_tensor(post_rstd[:], post_v[:], minus_half[:], ALU.pow).then_inc(post_ready, 1)

            def add_x1(b):
                pool.wait_ge(o_ln_ready, b + 1)
                xs = x_sb[:, bass.ts(b, NT), :]
                pool.tensor_tensor(xs, xs, o_ln[:], ALU.add).then_inc(x1_ready, 1)

            def rstd_both(n, cols=slice(None)):
                pool.wait_ge(both_var, n + 1)
                pool.tensor_tensor(ln_rstd[:, cols], ln_var[:, cols], minus_half[:, cols],
                                   ALU.pow).then_inc(both_ready, 1)

            def lo_weights(k):
                pool.wait_ge(w_hi_ready, k + 1)
                w = bass.ds(k, 1)
                pool.tensor_tensor(w_lo[:, w], w_raw[:, w], w_hi[:, w].bitcast(F32),
                                   ALU.subtract).then_inc(w_lo_ready, 1)

            pool.wait_ge(consts_ready, 1)
            rstd1(0)
            rstd1(1)
            copy_hm(0, 0)

            def step(b, p, weights=(), first=False, last=False):
                if not first:
                    rstd_post(b - 1)
                copy_hm(b + 1, 1 - p)
                for k in weights:
                    lo_weights(k)
                if last:
                    rstd_both(0)
                else:
                    rstd1(b + 2)
                if not first:
                    add_x1(b - 1)

            step(0, 0, [0, 1], first=True)
            step(1, 1, [2])
            with pool.Fori(1, B // 2 - 1) as i:
                step(2 * i, 0, [W_STEP * i, W_STEP * i + 1])
                step(2 * i + 1, 1, [W_STEP * i + 2])
            step(B - 2, 0, w_late, last=True)
            rstd_post(B - 2)
            add_x1(B - 2)

            def add_y(g):
                pool.wait_ge(y_ln_ready, g + 1)
                xs = x_sb[:, bass.ts(g, GT), :]
                pool.tensor_tensor(xs, xs, y_ln[:], ALU.add).then_inc(out_ready, 1)

            rstd_both(1, x_cols)
            rstd_post(B - 1)
            rstd_both(2, x_cols)
            add_x1(B - 1)
            with pool.Fori(2, G - 2) as g:
                rstd_both(g + 1)
                add_y(g - 2)
            for g in range(G - 2, G + 1):
                rstd_both(g + 1, y_cols)
                add_y(g - 2)
            rstd_both(G + 2, y_cols)

        @block.scalar
        def _(act):
            def normalise(b, h, halves=1):
                if h == 0:
                    act.wait_ge(ln1_ready, b + 1)
                for t in half_tiles[h]:
                    ins = act.activation(xn[:, t, :], x_sb[:, bass.ds(b * NT + t, 1), :],
                                         ACT.Identity, bias=ln_bias[:, t:t + 1], scale=ln_rstd[:, t:t + 1])
                ins.then_inc(xn_ready, halves)

            def copy_xt(b):
                for h in range(HALVES):
                    act.wait_ge(t_done, HALVES * b + h + 1)
                    act.copy(xt[:, h * BANK:(h + 1) * BANK], ps_prep[:, h, :]).then_inc(xt_ready, 1)

            def round_lat(b, p, h):
                act.wait_ge(lat_done, HALVES * b + h + 1)
                act.copy(lat_hh[p][:, h * BANK:(h + 1) * BANK], ps_prep[:, h, :]).then_inc(hi_ready, 1)

            def exp(b, j):
                for n, (jj, q, width) in enumerate(chunks):
                    if jj == j:
                        act.wait_ge(scores_done, NCH * b + n + 1)
                        at = probs_at[j] + q - j * P
                        act.activation(probs[:, at:at + width], ps_s[:, n % 2, 0:width], ACT.Exp,
                                       scale=SCALE).then_inc(probs_ready, 1)

            def copy_o(b, p, t):
                act.wait_ge(o_done, NT * b + t + 1)
                act.copy(o_sb[p][:, t, :], ps_o[:, t % 2, 0:C + 1]).then_inc(o_ready, 1)

            def copy_max_row(b, p, bank):
                for h in range(HALVES):
                    act.wait_ge(max_row_done, HALVES * b + h + 1)
                    act.mul(lat_hm[p][R:R + 1, h * BANK:(h + 1) * BANK], bank[R:R + 1, h, :],
                            -1.0).then_inc(max_row_ready, 1)

            def hi_weights(k):
                act.wait_ge(w_mlp_loaded, 16)
                w = bass.ds(k, 1)
                act.copy(w_hi[:, w], w_raw[:, w]).then_inc(w_hi_ready, 1)

            def round_xt(g):
                act.wait_ge(t2_done, g + 1)
                act.copy(xt_hi[:, 0, :], ps_t[:].rearrange("p t c -> p (t c)")).then_inc(xt2_hi_ready, 1)

            def step(b, p, first=False, reuse=True, prep=True, norm=True, weights=()):
                if prep and not first:
                    copy_xt(b + 1)
                exp(b, 0)
                if prep and not first:
                    round_lat(b + 1, 1 - p, 0)
                exp(b, 1)
                if prep and not first:
                    round_lat(b + 1, 1 - p, 1)
                exp(b, 2)
                if not prep:
                    round_xt(0)
                if reuse:
                    act.wait_ge(o_ln_ready, b - 1)
                copy_o(b, p, 0)
                exp(b, 3)
                copy_o(b, p, 1)
                for k in weights:
                    hi_weights(k)
                copy_o(b, p, 2)
                exp(b, 4)
                copy_o(b, p, 3)
                exp(b, 5)
                copy_o(b, p, 4)
                if norm:
                    normalise(b + 2, 0)
                exp(b, 6)
                if prep:
                    copy_o(b, p, 5)
                if norm:
                    normalise(b + 2, 1)
                exp(b, 7)
                if prep:
                    copy_o(b, p, 6)
                    copy_max_row(b + 1, 1 - p, ps_prep)
                    copy_o(b, p, 7)

            normalise(0, 0, HALVES)
            copy_xt(0)
            round_lat(0, 0, 0)
            round_lat(0, 0, 1)
            normalise(1, 0)
            normalise(1, 1)
            copy_xt(1)
            round_lat(1, 1, 0)
            round_lat(1, 1, 1)
            copy_max_row(0, 0, ps_o)
            step(0, 0, first=True, reuse=False, weights=[0, 1])
            step(1, 1, reuse=False, weights=[2])
            with act.Fori(1, B // 2 - 1) as i:
                step(2 * i, 0, weights=[W_STEP * i, W_STEP * i + 1])
                step(2 * i + 1, 1, weights=[W_STEP * i + 2])
            step(B - 2, 0, norm=False, weights=w_late)
            step(B - 1, 1, prep=False, norm=False)

            def silu(g, c):
                act.wait_ge(g_done, KC * g + c + 1)
                act.activation(gate[:, c % 2, :], ps_g[:, c % 2, :], ACT.Silu,
                               scale=scales[:, 0, c:c + 1]).then_inc(gate_ready, 1)

            def hi_h1(g, c):
                act.wait_ge(gated, KC * g + c + 1)
                act.copy(h1_hi[:, c, :], h1_full[:, c, :]).then_inc(h1_hi_ready, 1)

            def gelu2(g, c):
                act.wait_ge(h2_done, KC * g + c + 1)
                if c >= 2:
                    act.wait_ge(h2_ready, KC * g + c - 1)
                act.activation(h2_full[:, c % 2, :], ps_h[:, c % 2, :], ACT.Gelu,
                               scale=scales[:, 2, c:c + 1]).then_inc(h2_act, 1)

            def hi_h2(g, c):
                act.wait_ge(h2_act, KC * g + c + 1)
                act.copy(h2_hi[:, c, :], h2_full[:, c % 2, :]).then_inc(h2_hi_ready, 1)

            def gelu3(g, c):
                act.wait_ge(h3_done, KC * g + c + 1)
                if c >= 2:
                    act.wait_ge(h3_ready, KC * g + c - 1)
                act.activation(h3_full[:, c % 2, :], ps_h[:, c % 2, :], ACT.Gelu,
                               scale=scales[:, 3, c:c + 1]).then_inc(h3_act, 1)

            def hi_h3(g, c):
                act.wait_ge(h3_act, KC * g + c + 1)
                act.copy(h3_hi[:, c, :], h3_full[:, c % 2, :]).then_inc(h3_hi_ready, 1)

            def scale_y(g):
                act.wait_ge(y_done, g + 1)
                act.activation(yt[:], ps_y[:].rearrange("p t n -> p (t n)"), ACT.Copy,
                               scale=s_down_col[:, 0:1]).then_inc(yt_ready, 1)

            def mlp_step(g, has_t=True, has_3=True, has_y=True, last_o=False):
                silu(g, 0)
                silu(g, 1)
                if last_o:
                    copy_o(B - 1, 1, NT - 3)
                if has_3:
                    hi_h2(g - 1, KC - 1)
                if has_y:
                    scale_y(g - 2)
                hi_h1(g, 0)
                silu(g, 2)
                hi_h1(g, 1)
                silu(g, 3)
                if has_3:
                    gelu3(g - 1, 0)
                hi_h1(g, 2)
                if last_o:
                    copy_o(B - 1, 1, NT - 2)
                hi_h1(g, 3)
                if last_o:
                    copy_o(B - 1, 1, NT - 1)
                if has_3:
                    gelu3(g - 1, 1)
                    hi_h3(g - 1, 0)
                if has_t:
                    round_xt(g + 1)
                if has_3:
                    hi_h3(g - 1, 1)
                    for c in range(2, KC):
                        gelu3(g - 1, c)
                        hi_h3(g - 1, c)
                for c in range(KC):
                    gelu2(g, c)
                    if c < KC - 1:
                        hi_h2(g, c)

            act.wait_ge(s_loaded, 32)
            mlp_step(0, has_3=False, has_y=False, last_o=True)
            mlp_step(1, has_y=False)
            with act.Fori(2, G - 1) as g:
                mlp_step(g)
            mlp_step(G - 1, has_t=False)
            hi_h2(G - 1, KC - 1)
            scale_y(G - 2)
            for c in range(KC):
                gelu3(G - 1, c)
                hi_h3(G - 1, c)
            scale_y(G - 1)

        @block.vector
        def _(v):
            def setup():
                v.wait_ge(w_attn_loaded, 80)
                v.tensor_copy(b_v_bc[:], b_v_col[:].to_broadcast([P, P])).then_inc(setup_dve, 1)
                v.wait_ge(setup_pe, 1)
                v.tensor_copy(w_vo[:], ps_prep[:, 0, 0:P]).then_inc(setup_dve, 1)
                v.wait_ge(setup_pe, 2)
                v.tensor_tensor(b_vo_bc[:], ps_prep[:, 1, 0:P], b_o_bc[:], ALU.add).then_inc(setup_dve, 1)

            def ln1_stats(b, half, first=False):
                if first:
                    v.wait_ge(x0_loaded[half], 16)
                elif half == 0:
                    v.wait_ge(x_loaded, 16 * b)
                for t in half_tiles[half]:
                    ins = v.bn_stats(bn[:, t, :], x_sb[:, bass.ds(b * NT + t, 1), :])
                ins.then_inc(ln1_step, 1)

            def ln1_variance(b):
                v.wait_ge(ln1_step, LN1_STEPS * b + 2)
                aggregate(v, Steps(v, ln1_step, LN1_STEPS * b + 2), bn[:], ln_mean[:], ln_var[:],
                          ln_t[:], EPS).then_inc(ln1_var, 1)

            def ln1_scale(b):
                v.wait_ge(ln1_rstd, b + 1)
                v.scalar_tensor_tensor(out=ln_bias[:], in0=ln_mean[:], scalar=-1.0, in1=ln_rstd[:],
                                       op0=ALU.mult, op1=ALU.mult).then_inc(ln1_ready, 1)

            def lo_lat(b, p):
                for h in range(HALVES):
                    s = slice(h * BANK, (h + 1) * BANK)
                    v.wait_ge(hi_ready, HALVES * b + h + 1)
                    v.tensor_copy(lat_hl[p][0:R, s], lat_hh[p][0:R, s])
                    v.tensor_tensor(lat_hl[p][R:P, s], ps_prep[R:P, h, :],
                                    lat_hh[p][R:P, s].bitcast(F32), ALU.subtract)
                    v.tensor_tensor(lat_l1[p][0:R, s], ps_prep[0:R, h, :],
                                    lat_hh[p][0:R, s].bitcast(F32), ALU.subtract).then_inc(lo_ready, 1)

            def bias_values(b, p, h):
                v.wait_ge(val_done, HALVES * b + h + 1)
                n = BANK // P
                v.tensor_tensor(values[p][:, h * n:(h + 1) * n, 0:C],
                                ps_prep[:, h, :].rearrange("p (t c) -> p t c", c=C),
                                b_vo_bc[:].unsqueeze(1).to_broadcast([P, n, C]),
                                ALU.add).then_inc(val_ready, 1)

            def take_max(b, n):
                t, k, width = max_chunks[n]
                v.wait_ge(max_scores_done, NMX * b + n + 1)
                v.reduce_max(row_max[:, k // BANK, t:t + 1], ps_max[:, n % 2, 0:width],
                             AX_X).then_inc(max_ready, 1)

            def join_max(b):
                v.wait_ge(max_ready, NMX * (b + 1))
                two = slice(BANK // P, NT)
                v.tensor_tensor(row_max[:, 0, two], row_max[:, 0, two], row_max[:, 1, two],
                                ALU.max).then_inc(max_joined, 1)

            def post_stats(b, p, tiles):
                for t in tiles:
                    v.wait_ge(o_ready, NT * b + t + 1)
                    ins = v.bn_stats(post_bn[:, t, :], o_sb[p][:, t, 0:C])
                return ins

            def post_variance(b, p, ins):
                st = Steps(v, post_step, POST_STEPS * b)
                st.then(ins)
                r = o_sb[p][:, :, C]
                v.scalar_tensor_tensor(out=post_r2[:], in0=r, scalar=EPS, in1=r,
                                       op0=ALU.mult, op1=ALU.mult)
                st.then(aggregate(v, st, post_bn[:], post_mean[:], post_v[:], post_t[:], 0.0))
                v.tensor_tensor(post_v[:], post_v[:], post_r2[:], ALU.add).then_inc(post_var, 1)

            def post_normalise(b, p, tiles):
                for t in tiles:
                    ins = v.tensor_scalar(o_ln[:, t, :], o_sb[p][:, t, 0:C], post_mean[:, t:t + 1],
                                          post_rstd[:, t:t + 1], ALU.subtract, ALU.mult)
                if tiles[-1] == NT - 1:
                    ins.then_inc(o_ln_ready, 1)

            def prep_step(b, p, first=False, last=False):
                if last:
                    x1_stats(0)
                    stats = x1_stats(1, at=GT)
                else:
                    ln1_stats(b + 2, 0)
                    ln1_stats(b + 2, 1)
                if not first:
                    post_variance(b - 1, 1 - p, post_stats(b - 1, 1 - p, range(NT - 2, NT)))
                lo_lat(b + 1, 1 - p)
                take_max(b + 1, 0)
                take_max(b + 1, 1)
                bias_values(b + 1, 1 - p, 0)
                bias_values(b + 1, 1 - p, 1)
                take_max(b + 1, 2)
                take_max(b + 1, 3)
                if last:
                    both_variance(0, stats)
                else:
                    ln1_variance(b + 2)
                take_max(b + 1, 4)
                take_max(b + 1, 5)
                take_max(b + 1, 6)
                if not last:
                    ln1_scale(b + 2)
                post_stats(b, p, range(0, 3))
                for n in range(7, 10):
                    take_max(b + 1, n)
                post_stats(b, p, range(3, 5))
                for n in range(10, NMX):
                    take_max(b + 1, n)
                join_max(b + 1)
                if not first:
                    v.wait_ge(post_ready, b)
                    post_normalise(b - 1, 1 - p, range(NT))
                post_stats(b, p, range(5, NT - 2))

            def x1_stats(g, at=0):
                for t in range(GT):
                    ins = v.bn_stats(bn[:, at + t, :], x_sb[:, bass.ds(g * GT + t, 1), :])
                return ins

            def both_variance(n, ins, cols=slice(None)):
                st = Steps(v, both_step, BOTH_STEPS * n)
                st.then(ins)
                aggregate(v, st, bn[:, cols], ln_mean[:, cols], ln_var[:, cols], ln_t[:, cols],
                          EPS).then_inc(both_var, 1)

            def normalise_x1(g, at=0):
                for t in range(GT):
                    a = at + t
                    ins = v.tensor_scalar(xn2[:, t, :], x_sb[:, bass.ds(g * GT + t, 1), :],
                                          ln_mean[:, a:a + 1], ln_rstd[:, a:a + 1],
                                          ALU.subtract, ALU.mult)
                ins.then_inc(xn2_ready, 1)

            def lo_xt(g):
                v.wait_ge(xt2_hi_ready, g + 1)
                v.tensor_tensor(xt_lo[:, 0, :], ps_t[:].rearrange("p t c -> p (t c)"),
                                xt_hi[:, 0, :].bitcast(F32), ALU.subtract).then_inc(xt2_ready, 1)

            def gate_h1(g, c):
                v.wait_ge(gate_ready, KC * g + c + 1)
                v.wait_ge(u_done, KC * g + c + 1)
                v.scalar_tensor_tensor(out=h1_full[:, c, :], in0=ps_u[:, c % 2, :],
                                       scalar=scales[:, 1, c:c + 1], in1=gate[:, c % 2, :],
                                       op0=ALU.mult, op1=ALU.mult).then_inc(gated, 1)

            def lo_h1(g, c):
                v.wait_ge(h1_hi_ready, KC * g + c + 1)
                v.tensor_tensor(h1_lo[:, c, :], h1_full[:, c, :], h1_hi[:, c, :].bitcast(F32),
                                ALU.subtract).then_inc(h1_ready, 1)

            def lo_h2(g, c):
                v.wait_ge(h2_hi_ready, KC * g + c + 1)
                v.tensor_tensor(h2_lo[:, c, :], h2_full[:, c % 2, :], h2_hi[:, c, :].bitcast(F32),
                                ALU.subtract).then_inc(h2_ready, 1)

            def lo_h3(g, c):
                v.wait_ge(h3_hi_ready, KC * g + c + 1)
                v.tensor_tensor(h3_lo[:, c, :], h3_full[:, c % 2, :], h3_hi[:, c, :].bitcast(F32),
                                ALU.subtract).then_inc(h3_ready, 1)

            def y_stats(g):
                v.wait_ge(y_back, g + 1)
                for t in range(GT):
                    ins = v.bn_stats(bn[:, GT + t, :], ps_y[:, t, :])
                return ins

            def normalise_y(g, first=False):
                if not first:
                    v.wait_ge(out_ready, g)
                for t in range(GT):
                    a = GT + t
                    ins = v.tensor_scalar(y_ln[:, t, :], ps_y[:, t, :], ln_mean[:, a:a + 1],
                                          ln_rstd[:, a:a + 1], ALU.subtract, ALU.mult)
                ins.then_inc(y_ln_ready, 1)

            def mlp_step(g, has_x=True, has_t=True, has_3=True, has_y=True, first_y=False,
                         wait_x1=False, last_stats=False, last_norm=False):
                gate_h1(g, 0)
                gate_h1(g, 1)
                if has_3:
                    lo_h2(g - 1, KC - 1)
                lo_h1(g, 0)
                gate_h1(g, 2)
                lo_h1(g, 1)
                gate_h1(g, 3)
                if not has_3:
                    lo_h1(g, 2)
                    lo_h1(g, 3)
                if wait_x1:
                    v.wait_ge(x1_ready, B)
                if has_x:
                    ins = x1_stats(g + 2)
                if has_y:
                    ins = y_stats(g - 2)
                cols = slice(None) if has_x and has_y else x_cols if has_x else y_cols
                both_variance(g + 1, ins, cols)
                if has_3:
                    lo_h3(g - 1, 0)
                    lo_h1(g, 2)
                    lo_h1(g, 3)
                    lo_h3(g - 1, 1)
                if has_t:
                    lo_xt(g + 1)
                v.wait_ge(both_ready, g + 2)
                if has_y:
                    normalise_y(g - 2, first_y)
                if has_3:
                    lo_h3(g - 1, 2)
                if has_x:
                    normalise_x1(g + 2)
                if has_3:
                    lo_h3(g - 1, 3)
                for c in range(KC - 1):
                    lo_h2(g, c)
                    if last_stats and c < 2:
                        ins = post_stats(B - 1, 1, half_tiles[c])
                        if c == 1:
                            post_variance(B - 1, 1, ins)
                    if last_norm and c < 2:
                        v.wait_ge(post_ready, B)
                        post_normalise(B - 1, 1, half_tiles[c])

            ln1_stats(0, 0, first=True)
            ln1_stats(0, 1, first=True)
            ln1_variance(0)
            setup()
            ln1_scale(0)
            for t in half_tiles[1]:
                ins = v.tensor_scalar(xn[:, t, :], x_sb[:, t, :], ln_mean[:, t:t + 1],
                                      ln_rstd[:, t:t + 1], ALU.subtract, ALU.mult)
            ins.then_inc(xn_dve_ready, 1)
            v.wait_ge(xn_ready, HALVES)
            ln1_stats(1, 0)
            ln1_stats(1, 1)
            ln1_variance(1)
            lo_lat(0, 0)
            for n in range(NMX):
                take_max(0, n)
                if n == 0:
                    ln1_scale(1)
                if n == 3:
                    bias_values(0, 0, 0)
                if n == 4:
                    bias_values(0, 0, 1)
            join_max(0)
            prep_step(0, 0, first=True)
            prep_step(1, 1)
            with v.Fori(1, B // 2 - 1) as i:
                for p in range(2):
                    prep_step(2 * i + p, p)
            prep_step(B - 2, 0, last=True)

            v.wait_ge(both_ready, 1)
            normalise_x1(0)
            v.wait_ge(w_lo_ready, WK)
            v.tensor_reduce(lo_max[:], w_lo[:].rearrange("p k n -> p (k n)").bitcast(U32),
                            AX_X, ALU.max).then_inc(flag_step, 1)
            post_variance(B - 2, 0, post_stats(B - 2, 0, range(NT - 2, NT)))
            v.wait_ge(flag_step, 2)
            v.tensor_scalar(lo_flag[:], ps_prep[0:1, 1, 0:1], 0.0, None,
                            ALU.is_gt).then_inc(flag_step, 1)
            lo_xt(0)
            normalise_x1(1, at=GT)
            v.wait_ge(post_ready, B - 1)
            post_normalise(B - 2, 0, range(NT))

            v.wait_ge(s_loaded, 32)
            mlp_step(0, has_3=False, has_y=False, last_stats=True)
            mlp_step(1, has_y=False, last_norm=True)
            mlp_step(2, first_y=True, wait_x1=True)
            with v.Fori(3, G - 2) as g:
                mlp_step(g)
            mlp_step(G - 2, has_x=False)
            mlp_step(G - 1, has_x=False, has_t=False)
            lo_h2(G - 1, KC - 1)
            both_variance(G + 1, y_stats(G - 2), y_cols)
            lo_h3(G - 1, 0)
            lo_h3(G - 1, 1)
            v.wait_ge(both_ready, G + 2)
            normalise_y(G - 2)
            lo_h3(G - 1, 2)
            lo_h3(G - 1, 3)
            both_variance(G + 2, y_stats(G - 1), y_cols)
            v.wait_ge(both_ready, G + 3)
            normalise_y(G - 1)
            v.wait_ge(y_ln_ready, G)
            xs = x_sb[:, (G - 1) * GT:G * GT, :]
            v.tensor_tensor(xs, xs, y_ln[:], ALU.add).then_inc(last_out_ready, 1)

        @block.tensor
        def _(pe):
            pe.wait_ge(consts_ready, 1)
            pe.wait_ge(w_attn_loaded, 80)
            pe.matmul(ps_prep[:, 0, 0:P], w_v_sb[:], w_o_sb[:], start=True, stop=True).then_inc(setup_pe, 1)
            pe.wait_ge(setup_dve, 1)
            pe.matmul(ps_prep[:, 1, 0:P], b_v_bc[:], w_o_sb[:], start=True, stop=True).then_inc(setup_pe, 1)
            pe.wait_ge(setup_dve, 3)

            def keep_clock(n):
                for _ in range(n):
                    pe.matmul(ps_s[:, 0, 0:P], ident[:], ident[:], start=True, stop=True)

            def transpose_x(b, h):
                pe.wait_ge(xn_ready, HALVES * b + h + 1)
                for t in half_tiles[h]:
                    c = t * P - h * BANK
                    ins = pe.transpose(ps_prep[:, h, c:c + P], xn[:, t, :], ident[:])
                ins.then_inc(t_done, 1)

            def latents(b, h):
                pe.wait_ge(xt_ready, HALVES * b + h + 1)
                pe.matmul(ps_prep[:, h, :], w_basis[:], xt[:, h * BANK:(h + 1) * BANK],
                          start=True, stop=True).then_inc(lat_done, 1)

            def make_values(b, h):
                pe.wait_ge(lo_ready, HALVES * b + h + 1)
                for t in half_tiles[h]:
                    c = t * P - h * BANK
                    ins = pe.matmul(ps_prep[:, h, c:c + P], xt[:, t * P:(t + 1) * P], w_vo[:],
                                    start=True, stop=True)
                ins.then_inc(val_done, 1)

            def max_scores(b, p, n):
                t, k, width = max_chunks[n]
                if n == 0:
                    pe.wait_ge(hi_ready, HALVES * (b + 1))
                    pe.wait_ge(lo_ready, HALVES * b + 1)
                if n == 1:
                    pe.wait_ge(lo_ready, HALVES * (b + 1))
                if n >= 2:
                    pe.wait_ge(max_ready, NMX * b + n - 1)
                end = (t + 1) * P
                own = k + width == end
                ins = pe.matmul(ps_max[:, n % 2, 0:width], lat_hh[p][:, t * P:end],
                                lat_hl[p][:, k:k + width], start=True, stop=not own)
                if own:
                    ins = pe.matmul(ps_max[:, n % 2, width - P:width], ident_bf[:], mask_q[:],
                                    start=False, stop=True)
                ins.then_inc(max_scores_done, 1)

            def lay_max(b, bank):
                pe.wait_ge(max_joined, b + 1)
                pe.wait_ge(val_ready, HALVES * (b + 1))
                for t in range(NT):
                    h, c = divmod(t * P, BANK)
                    ins = pe.matmul(bank[R:R + 1, h, c:c + P], row_max[:, 0, t:t + 1], ident[:],
                                    start=True, stop=True)
                    if c + P == BANK:
                        ins.then_inc(max_row_done, 1)

            def scores(b, p, j):
                if j == 0:
                    pe.wait_ge(max_row_ready, HALVES * (b + 1))
                    pe.wait_ge(hm_ready, HALVES * (b + 1))
                for n, (jj, q, width) in enumerate(chunks):
                    if jj != j:
                        continue
                    if n >= 2:
                        pe.wait_ge(probs_ready, NCH * b + n - 1)
                    own = q == j * P
                    k = slice(j * P, (j + 1) * P)
                    pe.matmul(ps_s[:, n % 2, 0:width], lat_hh[p][:, k], lat_hl[p][:, q:q + width],
                              start=True, stop=False)
                    ins = pe.matmul(ps_s[:, n % 2, 0:width], lat_l1[p][:, k], lat_hm[p][:, q:q + width],
                                    start=False, stop=not own)
                    if own:
                        ins = pe.matmul(ps_s[:, n % 2, 0:P], ident_bf[:], mask_k[:], start=False, stop=True)
                    ins.then_inc(scores_done, 1)

            def attend(b, p, t, begin=0, end=NT):
                end = min(end, t + 1)
                pe.wait_ge(probs_ready, NCH * b + chunks_to[end - 1])
                if t >= 2 and begin == 0:
                    pe.wait_ge(o_ready, NT * b + t - 1)
                for j in range(begin, end):
                    at = probs_at[j] + (t - j) * P
                    ins = pe.matmul(ps_o[:, t % 2, 0:C + 1], probs[:, at:at + P], values[p][:, j, :],
                                    start=(j == 0), stop=(j == t))
                if end == t + 1:
                    ins.then_inc(o_done, 1)

            def prep_step(b, p, first=False):
                def maxima(*ns):
                    for n in ns:
                        max_scores(b + 1, 1 - p, n)

                if not first:
                    pe.wait_ge(max_row_ready, HALVES * (b + 1))
                    transpose_x(b + 1, 0)
                    transpose_x(b + 1, 1)
                scores(b, p, 0)
                if not first:
                    latents(b + 1, 0)
                scores(b, p, 1)
                if not first:
                    latents(b + 1, 1)
                scores(b, p, 2)
                attend(b, p, 0)
                attend(b, p, 1)
                scores(b, p, 3)
                attend(b, p, 2)
                maxima(0, 1)
                make_values(b + 1, 0)
                make_values(b + 1, 1)
                maxima(2, 3)
                scores(b, p, 4)
                attend(b, p, 3)
                maxima(4, 5)
                attend(b, p, 4)
                maxima(6)
                scores(b, p, 5)
                maxima(7)
                scores(b, p, 6)
                maxima(8)
                attend(b, p, 5)
                maxima(9, 10)
                attend(b, p, 6)
                maxima(11)
                scores(b, p, 7)
                attend(b, p, 7, end=2)
                lay_max(b + 1, ps_prep)
                attend(b, p, 7, begin=2)

            keep_clock(7)
            transpose_x(0, 0)
            pe.wait_ge(xn_dve_ready, 1)
            transpose_x(0, 1)
            latents(0, 0)
            latents(0, 1)
            keep_clock(8)
            for n in range(NMX):
                max_scores(0, 0, n)
                if n == 3:
                    make_values(0, 0)
                if n == 4:
                    make_values(0, 1)
                if 6 <= n < 8:
                    pe.wait_ge(val_ready, n - 5)
                    transpose_x(1, n - 6)
                if 8 <= n < 10:
                    latents(1, n - 8)
            lay_max(0, ps_o)
            prep_step(0, 0, first=True)
            prep_step(1, 1)
            with pe.Fori(1, B // 2 - 1) as i:
                for p in range(2):
                    prep_step(2 * i + p, p)
            prep_step(B - 2, 0)

            def transpose_x1(g):
                pe.wait_ge(xn2_ready, g + 1)
                for t in range(GT):
                    ins = pe.transpose(ps_t[:, t, :], xn2[:, t, :], ident[:])
                ins.then_inc(t2_done, 1)

            last = B - 1
            scores(last, 1, 0)
            scores(last, 1, 1)
            transpose_x1(0)
            for t in range(NT - 3):
                attend(last, 1, t)
                scores(last, 1, t + 2)
                if t == 3:
                    pe.wait_ge(flag_step, 1)
                    pe.matmul(ps_prep[0:1, 1, 0:1], lo_max[:], ones[:, 0:1], start=True,
                              stop=True).then_inc(flag_step, 1)
            scores(last, 1, NT - 1)
            pe.wait_ge(flag_step, 3)
            any_lo = pe.value_load(lo_flag[0:1, 0:1], min_val=0, max_val=1)

            def product(bank, weights, hi, lo, general, ready=None, before=0):
                for k, (chunk, cols) in enumerate(weights):
                    if ready is not None:
                        pe.wait_ge(ready, before + k + 1)
                    passes = [(w_hi, hi), (w_hi, lo)] + ([(w_lo, hi)] if general else [])
                    for n, (w, h) in enumerate(passes):
                        ins = pe.matmul(bank, w[:, chunk, cols], h[:, k, :], start=(k == 0 and n == 0),
                                        stop=(k == len(weights) - 1 and n == len(passes) - 1))
                return ins

            def columns(c):
                return slice(c * P, (c + 1) * P)

            def up(g, c, general):
                if c == 0:
                    pe.wait_ge(xt2_ready, g + 1)
                if c >= 2:
                    pe.wait_ge(gated, KC * g + c - 1)
                product(ps_g[:, c % 2, :], [(W1, columns(c))], xt_hi, xt_lo, general).then_inc(g_done, 1)
                product(ps_u[:, c % 2, :], [(W2, columns(c))], xt_hi, xt_lo, general).then_inc(u_done, 1)

            def hidden2(g, general, first=False):
                for c in range(KC):
                    if first and c < 2:
                        pe.wait_ge(o_ready, NT * B - 1 + c)
                    if c >= 2:
                        pe.wait_ge(h2_act, KC * g + c - 1)
                    elif not first:
                        pe.wait_ge(h3_act, KC * g + c - 1)
                    product(ps_h[:, c % 2, :], [(WH1 + k, columns(c)) for k in range(KC)], h1_hi, h1_lo,
                            general, h1_ready if c == 0 else None, KC * g).then_inc(h2_done, 1)

            def hidden3(g, c, general):
                if c < 2:
                    pe.wait_ge(h2_act, KC * g + c + 3)
                else:
                    pe.wait_ge(h3_act, KC * g + c - 1)
                product(ps_h[:, c % 2, :], [(WH2 + k, columns(c)) for k in range(KC)], h2_hi, h2_lo,
                        general, h2_ready if c == 0 else None, KC * g).then_inc(h3_done, 1)

            def down(g, general, first=False):
                if not first:
                    pe.wait_ge(y_ln_ready, g)
                product(ps_y[:].rearrange("p t n -> p (t n)"), [(W3, columns(k)) for k in range(KC)],
                        h3_hi, h3_lo, general, h3_ready, KC * g).then_inc(y_done, 1)

            def transpose_y(g):
                pe.wait_ge(yt_ready, g + 1)
                for t in range(GT):
                    ins = pe.transpose(ps_y[:, t, :], yt[:, t * P:(t + 1) * P], ident[:])
                ins.then_inc(y_back, 1)

            def mlp_step(g, general, has_t=True, has_3=True, has_y=True, first=False):
                if first:
                    pe.wait_ge(probs_ready, NCH * B)
                up(g, 0, general)
                up(g, 1, general)
                if first:
                    attend(last, 1, NT - 3)
                if has_t:
                    transpose_x1(g + 1)
                up(g, 2, general)
                up(g, 3, general)
                if first:
                    attend(last, 1, NT - 2)
                    attend(last, 1, NT - 1)
                if has_y:
                    transpose_y(g - 2)
                if has_3:
                    for c in range(KC):
                        hidden3(g - 1, c, general)
                hidden2(g, general, first)
                if has_3:
                    down(g - 1, general, not has_y)

            def mlp(general):
                mlp_step(0, general, has_3=False, has_y=False, first=True)
                mlp_step(1, general, has_y=False)
                with pe.Fori(2, G - 1) as g:
                    mlp_step(g, general)
                mlp_step(G - 1, general, has_t=False)
                for c in range(KC):
                    hidden3(G - 1, c, general)
                    if c == 0:
                        transpose_y(G - 2)
                down(G - 1, general)
                transpose_y(G - 1)

            with pe.If(any_lo):
                mlp(True)
            with pe.Else():
                mlp(False)


def kernel(**inputs):
    import numpy as np
    import concourse.bacc as bacc
    from concourse import mybir as mb
    from concourse.bass_utils import run_bass_kernel_spmd

    def a(name):
        return np.asarray(inputs[name])

    wb = a("L0_attn_W_basis").T
    names = ("w1", "w2", "h1", "h2")
    w3 = a("L0_ffn_w3_w").T.reshape(-1, 128, 128).transpose(1, 0, 2).reshape(128, -1)
    in_map = {
        "x": a("L0_attn_hidden_states"),
        "w_basis_dup_t": np.concatenate([wb, wb], axis=1),
        "w_v": a("L0_attn_W_v"),
        "w_o_t": a("L0_attn_W_o").T,
        "b_v": a("L0_attn_b_v").reshape(-1, 1),
        "b_o": a("L0_attn_b_o").reshape(1, -1),
        "w_mlp_t": np.concatenate([a(f"L0_ffn_{n}_w").T for n in names] + [w3], axis=0),
        "s_mlp": np.stack([a(f"L0_ffn_{n}_s").reshape(-1, 128).T for n in names], axis=1),
        "s_down": a("L0_ffn_w3_s").reshape(-1, 1),
    }
    nc = bacc.Bacc("TRN2", target_bir_lowering=False, num_devices=1)
    arrays, args = {}, []
    for name, value in in_map.items():
        value = np.ascontiguousarray(value)
        arrays[name + "_dram"] = value
        args.append(nc.dram_tensor(name + "_dram", value.shape, mb.dt.from_np(value.dtype),
                                   kind="ExternalInput").ap())
    x = in_map["x"]
    args.append(nc.dram_tensor("out_dram", x.shape, mb.dt.from_np(x.dtype), kind="ExternalOutput").ap())
    layer_kernel(nc, *args)
    r = run_bass_kernel_spmd(nc, [arrays], core_ids=[0])
    return r.results[0]["out_dram"]
```
